# Optimizing a Trainium2 kernel written in Bass

```python
import numpy as np
import jax
import jax.numpy as jnp

def _softmax(x, axis=-1):
    return jax.nn.softmax(x, axis=axis)

def _gelu(x):
    return jax.nn.gelu(x, approximate=True)

def _silu(x):
    return jax.nn.silu(x)

def _sigmoid(x):
    return jax.nn.sigmoid(x)

def _layernorm(x, axis=-1, eps=1e-05):
    m = jnp.mean(x, axis=axis, keepdims=True)
    v = jnp.var(x, axis=axis, keepdims=True)
    return (x - m) / jnp.sqrt(v + eps)

def _scatter_add(tgt, idx, src, axis=0):
    return tgt.at[idx].add(src)

def _segment_sum(src, seg, n):
    return jax.ops.segment_sum(src, seg, n)
kernel_name = 'mk_adaln_d1_jaxref_r8_675754'

def setup_inputs(seed: int=0):
    np.random.seed(seed)
    _w = jnp.asarray

    def _L0_attn_setup():
        import jax, jax.numpy as jnp
        import numpy as np
        B, S, H_DIM = (2, 256, 256)
        N_HEADS, D_HEAD = (16, 128)
        key = jax.random.key(seed)
        k1, k2, k3 = jax.random.split(key, 3)
        x = jax.random.normal(k1, (B, S, H_DIM), dtype=jnp.float32)
        w_qkv = jax.random.normal(k2, (H_DIM, 3 * N_HEADS * D_HEAD), dtype=jnp.float32) * 0.02
        w_o = jax.random.normal(k3, (N_HEADS * D_HEAD, H_DIM), dtype=jnp.float32) * 0.02
        return {'x': x, 'w_qkv': w_qkv, 'w_o': w_o}
    _L0_attn_in = _L0_attn_setup()

    def _L0_ffn_setup():
        import jax, jax.numpy as jnp
        import numpy as np
        DIM = 256
        HID = 704
        ZERO_POINT = 128.0

        def _qlinear(x, wq, scale):
            W = (wq.astype(jnp.float32) - ZERO_POINT) * scale[:, None]
            return jnp.einsum('bsd,hd->bsh', x, W)
        key = jax.random.key(seed)
        ks = jax.random.split(key, 7)
        B, S = (4, 256)
        sg = jax.random.uniform(ks[1], (HID,)) * (0.02 / np.sqrt(DIM)) + 0.0001
        su = jax.random.uniform(ks[3], (HID,)) * (0.02 / np.sqrt(DIM)) + 0.0001
        sd = jax.random.uniform(ks[5], (DIM,)) * (0.02 / np.sqrt(HID)) + 0.0001
        return {'x': jax.random.normal(ks[0], (B, S, DIM), dtype=jnp.float32), 'wq_gate': jax.random.randint(ks[2], (HID, DIM), 0, 32, dtype=jnp.int32), 's_gate': sg, 'wq_up': jax.random.randint(ks[4], (HID, DIM), 0, 32, dtype=jnp.int32), 's_up': su, 'wq_down': jax.random.randint(ks[6], (DIM, HID), 0, 32, dtype=jnp.int32), 's_down': sd}
    _L0_ffn_in = _L0_ffn_setup()
    _L0_c = _w((lambda *s: np.random.randn(*s).astype(np.float32) * 0.05)(2, 256))
    _L0_wmod = _w((lambda *s: np.random.randn(*s).astype(np.float32) * 0.05)(256, 6 * 256) * 256 ** (-0.5))
    _d = {'L0_attn_x': _L0_attn_in['x'], 'L0_attn_w_qkv': _L0_attn_in['w_qkv'], 'L0_attn_w_o': _L0_attn_in['w_o'], 'L0_ffn_wq_gate': _L0_ffn_in['wq_gate'], 'L0_ffn_s_gate': _L0_ffn_in['s_gate'], 'L0_ffn_wq_up': _L0_ffn_in['wq_up'], 'L0_ffn_s_up': _L0_ffn_in['s_up'], 'L0_ffn_wq_down': _L0_ffn_in['wq_down'], 'L0_ffn_s_down': _L0_ffn_in['s_down'], 'L0_c': _L0_c, 'L0_wmod': _L0_wmod}
    _x0 = _d['L0_attn_x']
    _d['L0_attn_x'] = jax.random.normal(jax.random.fold_in(jax.random.key(seed), 1), (2, 1024, 256), dtype=_x0.dtype)
    del _x0
    return _d

def reference(L0_attn_x, L0_attn_w_qkv, L0_attn_w_o, L0_ffn_wq_gate, L0_ffn_s_gate, L0_ffn_wq_up, L0_ffn_s_up, L0_ffn_wq_down, L0_ffn_s_down, L0_c, L0_wmod):

    def _L0_attn_ref(x, w_qkv, w_o):
        import jax, jax.numpy as jnp
        import numpy as np
        B, S, H_DIM = (2, 256, 256)
        N_HEADS, D_HEAD = (16, 128)
        b, s, _ = x.shape
        qkv = jnp.einsum('bsh,hf->bsf', x, w_qkv)
        qkv = qkv.reshape(b, s, 3, N_HEADS, D_HEAD)
        q, k, v = (qkv[:, :, 0], qkv[:, :, 1], qkv[:, :, 2])
        q = q.transpose(0, 2, 1, 3)
        k = k.transpose(0, 2, 1, 3)
        v = v.transpose(0, 2, 1, 3)
        scores = jnp.einsum('bhqd,bhkd->bhqk', q, k) / jnp.sqrt(jnp.float32(D_HEAD))
        probs = jax.nn.softmax(scores, axis=-1)
        values = jnp.einsum('bhqk,bhkd->bhkd', probs, v)
        values = values.transpose(0, 2, 1, 3).reshape(b, s, N_HEADS * D_HEAD)
        out = jnp.einsum('bsf,fh->bsh', values, w_o)
        return out

    def _L0_ffn_ref(x, wq_gate, s_gate, wq_up, s_up, wq_down, s_down):
        import jax, jax.numpy as jnp
        import numpy as np
        DIM = 256
        HID = 704
        ZERO_POINT = 128.0

        def _qlinear(x, wq, scale):
            W = (wq.astype(jnp.float32) - ZERO_POINT) * scale[:, None]
            return jnp.einsum('bsd,hd->bsh', x, W)
        gate = _qlinear(x, wq_gate, s_gate)
        gate = jax.nn.silu(gate)
        up = _qlinear(x, wq_up, s_up)
        return _qlinear(gate * up, wq_down, s_down)
    x = L0_attn_x
    mod = (_silu(L0_c) @ L0_wmod).reshape(L0_c.shape[0], 6, 1, -1)
    sa, ca, ga, sb, cb, gb = (mod[:, 0], mod[:, 1], mod[:, 2], mod[:, 3], mod[:, 4], mod[:, 5])
    ga = (2 * (ga >= 0) - 1) * jnp.maximum(jnp.abs(ga), 0.25)
    gb = (2 * (gb >= 0) - 1) * jnp.maximum(jnp.abs(gb), 0.25)
    h = _layernorm(x, axis=-1) * (1 + ca) + sa
    x = x + ga * _L0_attn_ref(h, L0_attn_w_qkv, L0_attn_w_o)
    h = _layernorm(x, axis=-1) * (1 + cb) + sb
    x = x + gb * _L0_ffn_ref(h, L0_ffn_wq_gate, L0_ffn_s_gate, L0_ffn_wq_up, L0_ffn_s_up, L0_ffn_wq_down, L0_ffn_s_down)
    return x

_drawn_inputs = setup_inputs


def setup_inputs(seed=0):
    import zlib

    import numpy as np

    out = dict(_drawn_inputs(seed))
    spreads = {}
    factors = {'L0_ffn_s_gate': 8.0, 'L0_ffn_s_up': 8.0, 'L0_ffn_s_down': 8.0}
    for name, (base, spread) in spreads.items():
        noise = np.random.default_rng([zlib.crc32(name.encode()), seed]).standard_normal(out[name].shape)
        drawn = base * np.exp(spread * noise) if base else spread * noise
        out[name] = jnp.asarray(drawn.astype(out[name].dtype))
    for name, factor in factors.items():
        out[name] = (out[name] * factor).astype(out[name].dtype)
    return out
```

```python
from contextlib import ExitStack

import concourse.bass as bass
from concourse import mybir

F32 = mybir.dt.float32
F32R = mybir.dt.float32r
I32 = mybir.dt.int32
ALU = mybir.AluOpType
ACT = mybir.ActivationFunctionType
AX = mybir.AxisListType

P = 128
BANK = 512
EPS = 1e-5
ZERO_POINT = 128.0
GATE_MIN = 0.25


def adaln_block(nc, x_d, w_qkv_d, w_o_d, wq_gate_d, s_gate_d, wq_up_d, s_up_d, wq_down_d, s_down_d,
                c_d, wmod_d, out_d):
    B, S, D = x_d.shape
    DH = 128
    NH = w_o_d.shape[0] // DH
    HID = wq_gate_d.shape[0]
    SCALE = float(DH) ** -0.5
    DC = D // P
    QT = S // P
    NT = B * QT
    PAIRS = NH // 2
    UNITS = 2 * B
    STEPS = UNITS * QT
    HF = HID // P
    HR = HID - HF * P
    HK = HF + 1
    GU = 2 * HF + 1
    TB = BANK // P
    NB = NT // TB
    assert B == 2 and D == 256 and S == 1024 and NH % 2 == 0 and HR == 64

    UNIT = [(0, 0), (1, 0), (0, 1), (1, 1)]
    YM = 3 * DC
    YSTEPS = 12
    PER = QT * YM // YSTEPS
    CSTEP = 3
    Y0 = CSTEP + 1
    YEND = {(YM * (i + 1) - 1) // PER: i for i in range(QT)}

    ctx = ExitStack()
    with ctx:
        def sb(name, shape, dt=F32):
            return ctx.enter_context(nc.sbuf_tensor(name, shape, dt))

        def pb(name, shape):
            return ctx.enter_context(nc.psum_tensor(name, shape, F32))

        def sem(name):
            return ctx.enter_context(nc.semaphore(name))

        x = sb("x", [P, NT, D])
        hTh = sb("hTh", [P, DC, B * S], F32R)
        hTl = sb("hTl", [P, DC, B * S], F32R)
        attn = sb("attn", [P, NT, D])
        qk = sb("qk", [P, 2, 4, S], F32R)
        prob = sb("prob", [P, 4, S])
        psumw = sb("psumw", [P, 2, S])
        praw = sb("praw", [P, 2, BANK])
        ysc = sb("ysc", [P, 2, 2 * D])
        wraw = sb("wraw", [P, 3, DC, 2 * DH])
        woraw = sb("woraw", [P, 2, D])
        wqkh = [sb(f"wqkh{a}", [P, 2, DC, DH], F32R) for a in range(2)]
        wqkl = [sb(f"wqkl{a}", [P, 2, DC, DH], F32R) for a in range(2)]
        woh = sb("woh", [P, 2, D], F32R)
        wol = sb("wol", [P, 2, D], F32R)
        wvTh = sb("wvTh", [P, 2, DC, P], F32R)
        wvTl = sb("wvTl", [P, 2, DC, P], F32R)
        mvoh = sb("mvoh", [P, DC, 2 * D], F32R)
        mvol = sb("mvol", [P, DC, 2 * D], F32R)
        wguh = sb("wguh", [P, DC, GU * P], F32R)
        wgul = sb("wgul", [P, DC, GU * P], F32R)
        wdh = sb("wdh", [P, HK, D], F32R)
        wdl = sb("wdl", [P, HK, D], F32R)
        wdraw = sb("wdraw", [P, DC, HID])
        ident = sb("ident", [P, P])
        ones = sb("ones", [P, 2])
        gates = sb("gates", [P, 2, B, D])
        modc = sb("modc", [P, 4, DC, B])
        cT = sb("cT", [P, DC, B])
        siluc = sb("siluc", [P, DC, B])
        sgu = sb("sgu", [P, GU])
        sdn = sb("sdn", [P, DC])
        stats = sb("stats", [P, NT, 6])
        mv = sb("mv", [P, NT, 2])
        std = sb("std", [P, NT])
        rstd = sb("rstd", [P, NT])
        nmax = sb("nmax", [P, 4])
        zsum = sb("zsum", [P, 4])
        rz = sb("rz", [P, 4])
        colsum = sb("colsum", [P, UNITS, QT])

        wmod = prob[:, 0:3, :].rearrange("p a n -> p (a n)").rearrange("p (c n) -> p c n", c=DC)
        htmp = prob[:, 3, :].rearrange("p (a n) -> p a n", a=2)
        xn = praw[:, :, :].rearrange("p a n -> p (a n)").rearrange("p (t d) -> p t d", t=TB)
        scbc = psumw[:, 0, 0:DC * B * P].rearrange("p (c b n) -> p c b n", c=DC, b=B)
        gtmp = psumw[:, 1, :].rearrange("p (g b d) -> p g b d", g=2, b=B)
        wgu_f = attn[:, 0:GU, :]
        wgu_i = attn[:, 0:GU, :].bitcast(I32)
        wd_i = wdraw[:, :, :].bitcast(I32)
        acth = qk[:, 0, 0:3, :].rearrange("p a n -> p (a n)").rearrange("p (k n) -> p k n", k=HK)
        actl = qk[:, 1, 0:3, :].rearrange("p a n -> p (a n)").rearrange("p (k n) -> p k n", k=HK)
        silg = prob[:, 0, :].rearrange("p (a n) -> p a n", a=2)
        act32 = prob[:, 1, :].rearrange("p (a n) -> p a n", a=2)

        score = [pb(f"score{i}", [P, 2, BANK]) for i in range(2)]
        proj = pb("proj", [P, BANK])
        misc = pb("misc", [P, BANK])
        ybank = [pb(f"ybank{i}", [P, BANK]) for i in range(2)]
        four = [score[0][:, 0, :], score[0][:, 1, :], score[1][:, 0, :], score[1][:, 1, :]]
        down = [ybank[0][:, 0:D], ybank[1][:, 0:D], proj[:, 0:D], misc[:, 0:D]]

        x_in = [sem(f"x_in{i}") for i in range(NB)]
        c_in, wmod_in, ffnw_in = sem("c_in"), sem("wmod_in"), sem("ffnw_in")
        wqkv_in, wo_in = sem("wqkv_in"), sem("wo_in")
        stored = sem("stored")
        const_done, pool_chain, dve_chain = sem("const_done"), sem("pool_chain"), sem("dve_chain")
        siluc_done, scbc_done, mod_mm, gate_mm, mod_done = (sem(n) for n in (
            "siluc_done", "scbc_done", "mod_mm", "gate_mm", "mod_done"))
        stats_done, std_done, xn_done = sem("stats_done"), sem("std_done"), sem("xn_done")
        xnT_mm, hT_hi, hT_lo = sem("xnT_mm"), sem("hT_hi"), sem("hT_lo")
        wqk_hi, wqk_lo, wo_hi, wo_lo = sem("wqk_hi"), sem("wqk_lo"), sem("wo_hi"), sem("wo_lo")
        proj_mm, proj_hi, proj_lo = sem("proj_mm"), sem("proj_hi"), sem("proj_lo")
        score_mm, max_done, exp_done, rz_done, acc_done = (sem(n) for n in (
            "score_mm", "max_done", "exp_done", "rz_done", "acc_done"))
        misc_mm, misc_hi, misc_free = sem("misc_mm"), sem("misc_hi"), sem("misc_free")
        y_mm, y_scaled, y_added = sem("y_mm"), sem("y_scaled"), sem("y_added")
        ffnw_f, ffnw_mm, ffnw_hi, ffnw_lo, attn_zero = (sem(n) for n in (
            "ffnw_f", "ffnw_mm", "ffnw_hi", "ffnw_lo", "attn_zero"))
        gu_mm, sil_done, act_done, act_hi, act_lo = (sem(n) for n in (
            "gu_mm", "sil_done", "act_done", "act_hi", "act_lo"))
        down_mm, down_free, out_done = sem("down_mm"), sem("down_free"), sem("out_done")

        def f32(ap):
            return ap.bitcast(F32)

        def y_count(p, phase):
            return p * 2 * QT + (0 if phase else -QT)

        MISC = 7
        M_T, M_C0, M_M0, M_M1, M_C1, M_C2, M_C3 = range(MISC)

        def misc_n(p, what):
            return p * MISC + what + 1

        def y_tile(k):
            return YEND.get(k)

        T_AT, M0_AT, M1_AT = (0, 5), (1, 7), (2, 1)
        T_EV, M0_EV, M1_EV = (0, 6), (2, 0), (2, 2)

        ffn_banks = [("gu", c, s, min(4, GU - s)) for c in range(DC) for s in range(0, GU, 4)]
        ffn_banks += [("dn", k, min(2, HF - k), P) for k in range(0, HF, 2)] + [("dn", HF, 1, HR)]
        assert len(ffn_banks) <= YSTEPS

        def ffn_views(bank):
            if bank[0] == "gu":
                _, c, s, n = bank
                return P, n * P, wguh[:, c, s * P:(s + n) * P], wgul[:, c, s * P:(s + n) * P]
            _, k, n, rows = bank
            return (rows, n * D, wdh[0:rows, k:k + n, :].rearrange("p k d -> p (k d)"),
                    wdl[0:rows, k:k + n, :].rearrange("p k d -> p (k d)"))

        qkv_v = w_qkv_d.rearrange("(c p) (w n) -> w p c n", p=P, w=3)
        wo_v = w_o_d.rearrange("(h d) n -> d h n", d=DH)
        x_v = x_d.rearrange("b (t p) d -> p (b t) d", p=P)
        out_v = out_d.rearrange("b (t p) d -> p (b t) d", p=P)

        block = ctx.enter_context(nc.Block())

        @block.sync
        def _(sp):
            def load_qkv(p):
                for w in range(3):
                    sp.dma_start(wraw[:, w, :, :], qkv_v[w, :, :, bass.ds(p * (2 * DH), 2 * DH)])\
                      .then_inc(wqkv_in, 16)

            def load_wo(p):
                sp.dma_start(woraw[:, :, :], wo_v[:, bass.ds(p * 2, 2), :]).then_inc(wo_in, 16)

            with nc.allow_non_contiguous_dma(reason="a few hundred words, once"):
                for c in range(DC):
                    sp.dma_start(cT[:, c, :], c_d[:, c * P:(c + 1) * P].rearrange("b p -> p b"))\
                      .then_inc(c_in, 16)
            for n in range(NB):
                sp.dma_start(x[:, n * TB:(n + 1) * TB, :], x_v[:, n * TB:(n + 1) * TB, :])\
                  .then_inc(x_in[n], 16)
                if n == 0:
                    sp.dma_start(wmod, wmod_d.rearrange("(c p) n -> p c n", p=P)).then_inc(wmod_in, 16)
            load_qkv(0)
            load_wo(0)
            for n, (w_d, s_d) in enumerate(((wq_gate_d, s_gate_d), (wq_up_d, s_up_d))):
                rem = slice(n * HR, (n + 1) * HR)
                sp.dma_start(wgu_i[:, n * HF:(n + 1) * HF, :],
                             w_d[0:HF * P, :].rearrange("(k p) d -> p k d", p=P)).then_inc(ffnw_in, 16)
                sp.dma_start(wgu_i[rem, 2 * HF, :], w_d[HF * P:HID, :]).then_inc(ffnw_in, 16)
                with nc.allow_non_contiguous_dma(reason="one scale per row"):
                    sp.dma_start(sgu[:, n * HF:(n + 1) * HF],
                                 s_d[0:HF * P].rearrange("(k p) -> p k", p=P)).then_inc(ffnw_in, 16)
                    sp.dma_start(sgu[rem, 2 * HF:GU],
                                 s_d[HF * P:HID].rearrange("(p a) -> p a", a=1)).then_inc(ffnw_in, 16)
            sp.dma_start(wd_i, wq_down_d.rearrange("(c p) k -> p c k", p=P)).then_inc(ffnw_in, 16)
            with nc.allow_non_contiguous_dma(reason="one scale per row"):
                sp.dma_start(sdn[:, :], s_down_d.rearrange("(c p) -> p c", p=P)).then_inc(ffnw_in, 16)

            def next_pair(p):
                sp.wait_ge(misc_mm, misc_n(p, M_T))
                sp.wait_ge(wqk_lo, p * 2 + 2)
                load_qkv(p + 1)
                sp.wait_ge(wo_lo, p + 1)
                load_wo(p + 1)

            with sp.Fori(0, PAIRS - 1) as p:
                next_pair(p)
            for t in range(NT):
                sp.wait_ge(out_done, t + 1)
                sp.dma_start(out_v[:, t, :], attn[:, t, :]).then_inc(stored, 16)
            sp.wait_ge(stored, 16 * NT)

        @block.gpsimd
        def _(pool):
            nc.gpsimd.memset(ident[:, :], 0.0).then_inc(pool_chain, 1)
            nc.gpsimd.memset(ones[:, :], 1.0).then_inc(const_done, 1)
            pool.wait_ge(pool_chain, 1)
            nc.gpsimd.affine_select(out=ident[:, :], in_=ident[:, :], compare_op=ALU.not_equal, fill=1.0,
                                    base=0, pattern=[[-1, P]], channel_multiplier=1).then_inc(const_done, 1)

            def split_wqk(p, a):
                pool.wait_ge(wqk_hi, p * 2 + a + 1)
                nc.gpsimd.tensor_tensor(wqkl[a][:, :, :, :], wraw[:, 0:2, :, a * DH:(a + 1) * DH],
                                        f32(wqkh[a][:, :, :, :]), ALU.subtract).then_inc(wqk_lo, 1)

            def split_wo(p):
                pool.wait_ge(wo_hi, p + 1)
                nc.gpsimd.tensor_tensor(wol[:, :, :], woraw[:, :, :], f32(woh[:, :, :]),
                                        ALU.subtract).then_inc(wo_lo, 1)

            def proj_split(n, par, g):
                w, blk = g // 2, g % 2
                cols = slice(blk * BANK, (blk + 1) * BANK)
                pool.wait_ge(proj_hi, n + 1)
                nc.gpsimd.tensor_tensor(qk[:, par, 2 * w + 1, cols], praw[:, g % 2, :],
                                        f32(qk[:, par, 2 * w, cols]), ALU.subtract).then_inc(proj_lo, 1)

            def y_add(n, i, b):
                t = b * QT + i
                pool.wait_ge(y_scaled, n + 1)
                if i == 0:
                    pool.wait_ge(attn_zero, 1)
                for a in range(2):
                    if a:
                        pool.wait_ge(y_added, n * 2 + 1)
                    nc.gpsimd.tensor_tensor(attn[:, t, :], attn[:, t, :], ysc[:, i % 2, a * D:(a + 1) * D],
                                            ALU.add).then_inc(y_added, 1)

            for a in range(2):
                split_wqk(0, a)
            for g in range(4):
                proj_split(g, 0, g)
            pool.wait_ge(ffnw_in, 10 * 16)
            for s in range(GU):
                nc.gpsimd.tensor_scalar(wgu_f[:, s, :], wgu_i[:, s, :], -ZERO_POINT, sgu[:, s:s + 1],
                                        ALU.add, ALU.mult).then_inc(ffnw_f, 1)
            for c in range(DC):
                nc.gpsimd.tensor_scalar(wdraw[:, c, :], wd_i[:, c, :], -ZERO_POINT, sdn[:, c:c + 1],
                                        ALU.add, ALU.mult).then_inc(ffnw_f, 1)

            def pair(p, first, last):
                for t in range(STEPS):
                    j, qt = t // QT, t % QT
                    if qt % 2 == 1 and not (last and j == UNITS - 1):
                        g = qt // 2
                        proj_split(p * (4 * UNITS) + 4 * (j + 1) + g, (j + 1) % 2, g)
                    if (j, qt) == (1, 1):
                        split_wo(p)
                    if (j, qt) in ((2, 5), (3, 5)) and not last:
                        split_wqk(p + 1, j - 2)
                    phase = j // 2
                    k = t - phase * 2 * QT - Y0
                    if first and (j, qt) == (2, 0):
                        pool.wait_ge(ffnw_mm, len(ffn_banks))
                        nc.gpsimd.memset(attn[:, :, :], 0.0).then_inc(attn_zero, 1)
                    if k >= 0 and y_tile(k) is not None and not (first and phase == 0):
                        y_add(y_count(p, phase) + y_tile(k), y_tile(k), 1 - phase)

            pair(0, True, False)
            with pool.Fori(1, PAIRS - 1) as p:
                pair(p, False, False)
            pair(PAIRS - 1, False, True)
            for i in range(QT):
                y_add(y_count(PAIRS, 0) + i, i, 1)
            for n in range(NB * HK):
                k = n % HK
                rows = P if k < HF else HR
                pool.wait_ge(act_hi, n + 1)
                nc.gpsimd.tensor_tensor(actl[0:rows, k, :], act32[0:rows, n % 2, :],
                                        f32(acth[0:rows, k, :]), ALU.subtract).then_inc(act_lo, 1)

        @block.scalar
        def _(act):
            act.wait_ge(c_in, 16 * DC)
            nc.scalar.activation(siluc[:, :, :], cT[:, :, :], ACT.Silu).then_inc(siluc_done, 1)

            def split_wqk(p, a):
                act.wait_ge(wqkv_in, p * 48 + 48)
                nc.scalar.activation(wqkh[a][:, :, :, :], wraw[:, 0:2, :, a * DH:(a + 1) * DH], ACT.Copy)\
                  .then_inc(wqk_hi, 1)

            def hT_block(m, n, c):
                i = m * NB * DC + n * DC + c
                b = n // (NB // B)
                cols = slice(n * BANK, (n + 1) * BANK)
                act.wait_ge(xnT_mm, i + 1)
                if i >= 2:
                    act.wait_ge(hT_lo, i - 1)
                for dst in (htmp[:, i % 2, :], hTh[:, c, cols]):
                    last = nc.scalar.activation(dst, four[i % 4], ACT.Identity,
                                                bias=modc[:, 2 * m, c, b:b + 1],
                                                scale=modc[:, 2 * m + 1, c, b:b + 1])
                last.then_inc(hT_hi, 1)

            def sqrt_var(n, tiles):
                act.wait_ge(stats_done, n)
                nc.scalar.activation(std[:, tiles], mv[:, tiles, 1], ACT.Sqrt).then_inc(std_done, 1)

            sqrt_var(1, slice(0, NT))
            act.wait_ge(mod_done, 1)
            for n in range(NB):
                for c in range(DC):
                    hT_block(0, n, c)
                if n == 0:
                    for a in range(2):
                        split_wqk(0, a)

            def proj_out(n, par, g):
                w, blk = g // 2, g % 2
                act.wait_ge(proj_mm, n + 1)
                if not isinstance(n, int) or n >= 2:
                    act.wait_ge(proj_lo, n - 1)
                for dst in (praw[:, g % 2, :], qk[:, par, 2 * w, blk * BANK:(blk + 1) * BANK]):
                    last = nc.scalar.activation(dst, proj[:, :], ACT.Copy, scale=1.0 if w else SCALE)
                last.then_inc(proj_hi, 1)

            act.wait_ge(xnT_mm, NB * DC)
            for g in range(4):
                proj_out(g, 0, g)

            def y_scale(n, i, b):
                act.wait_ge(y_mm, n + 1)
                if not isinstance(n, int) or n >= 2:
                    act.wait_ge(y_added, n * 2 - 2)
                for a in range(2):
                    last = nc.scalar.activation(ysc[:, i % 2, a * D:(a + 1) * D],
                                                ybank[i % 2][:, a * D:(a + 1) * D], ACT.Copy,
                                                scale=colsum[:, 2 * b + a, i:i + 1])
                last.then_inc(y_scaled, 1)

            def pair(p, first, last):
                for t in range(STEPS):
                    j, qt = t // QT, t % QT
                    phase = (t - 1) // (2 * QT)
                    k = t - 1 - phase * 2 * QT - Y0
                    if t > 0 and k >= 0:
                        if y_tile(k) is not None and not (first and phase == 0):
                            y_scale(y_count(p, phase) + y_tile(k), y_tile(k), 1 - phase)
                        if first and phase == 0 and k < len(ffn_banks):
                            rows, cols, hi, _ = ffn_views(ffn_banks[k])
                            act.wait_ge(ffnw_mm, k + 1)
                            nc.scalar.activation(hi, ybank[k % 2][0:rows, 0:cols], ACT.Copy)\
                              .then_inc(ffnw_hi, 1)
                    if (j, qt) == T_EV:
                        act.wait_ge(misc_mm, misc_n(p, M_T))
                        nc.scalar.activation(wvTh[:, :, :, :], misc[:, :], ACT.Copy).then_inc(misc_hi, 1)
                    if (j, qt) == (1, 1):
                        act.wait_ge(wo_in, p * 16 + 16)
                        nc.scalar.activation(woh[:, :, :], woraw[:, :, :], ACT.Copy).then_inc(wo_hi, 1)
                    for c, at, what in ((0, M0_EV, M_M0), (1, M1_EV, M_M1)):
                        if (j, qt) == at:
                            act.wait_ge(misc_mm, misc_n(p, what))
                            nc.scalar.activation(mvoh[:, c, :], misc[:, :], ACT.Copy).then_inc(misc_hi, 1)
                    if (j, qt) in ((2, 5), (3, 5)) and not last:
                        split_wqk(p + 1, j - 2)
                    if qt % 2 == 1 and not (last and j == UNITS - 1):
                        g = qt // 2
                        proj_out(p * (4 * UNITS) + 4 * (j + 1) + g, (j + 1) % 2, g)
                    act.wait_ge(max_done, p * STEPS + t + 1)
                    if not (first and t < 4):
                        act.wait_ge(acc_done, p * STEPS + t - 3)
                    nc.scalar.activation(prob[:, t % 4, :], score[t % 2][:, :, :], ACT.Exp,
                                         bias=nmax[:, t % 4:t % 4 + 1], scale=1.0,
                                         accum_out=zsum[:, t % 4:t % 4 + 1]).then_inc(exp_done, 1)
                y_scale(y_count(p, 1) + QT - 1, QT - 1, 0)

            pair(0, True, False)
            with act.Fori(1, PAIRS - 1) as p:
                pair(p, False, False)
            pair(PAIRS - 1, False, True)
            sqrt_var(2, slice(0, QT))
            for i in range(QT):
                y_scale(y_count(PAIRS, 0) + i, i, 1)

            def ffn_act(n):
                k = n % HK
                rows = P if k < HF else HR
                act.wait_ge(gu_mm, n + 1)
                if n >= 2:
                    act.wait_ge(act_done, n - 1)
                nc.scalar.activation(silg[0:rows, n % 2, :], four[2 * (n % 2)][0:rows, :], ACT.Silu)\
                  .then_inc(sil_done, 1)

            def ffn_hi(n):
                k = n % HK
                rows = P if k < HF else HR
                act.wait_ge(act_done, n + 1)
                nc.scalar.activation(acth[0:rows, k, :], act32[0:rows, n % 2, :], ACT.Copy)\
                  .then_inc(act_hi, 1)

            for half in range(B):
                if half:
                    sqrt_var(3, slice(QT, NT))
                for nn in range(NB // B):
                    for c in range(DC):
                        hT_block(1, half * (NB // B) + nn, c)
                for nn in range(NB // B):
                    base = (half * (NB // B) + nn) * HK
                    for k in range(HK):
                        ffn_act(base + k)
                        if k:
                            ffn_hi(base + k - 1)
                    ffn_hi(base + HK - 1)

        @block.tensor
        def _(pe):
            def three(out, stat_hi, stat_lo, mov_hi, mov_lo, start, stop):
                nc.tensor.matmul(out, stat_hi, mov_hi, start=start, stop=False)
                nc.tensor.matmul(out, stat_hi, mov_lo, start=False, stop=False)
                return nc.tensor.matmul(out, stat_lo, mov_hi, start=False, stop=stop)

            pe.wait_ge(siluc_done, 1)
            pe.wait_ge(wmod_in, 16)
            for n, kind in enumerate((0, 1, 3, 4)):
                for c2 in range(DC):
                    at = (n * DC + c2) * B
                    for c in range(DC):
                        last = nc.tensor.matmul(misc[:, at:at + B],
                                                wmod[:, c, kind * D + c2 * P:kind * D + (c2 + 1) * P],
                                                siluc[:, c, :], start=c == 0, stop=c == DC - 1)
            last.then_inc(mod_mm, 1)
            pe.wait_ge(scbc_done, 1)
            for n, kind in enumerate((2, 5)):
                for b in range(B):
                    for c in range(DC):
                        last = nc.tensor.matmul(ybank[n][:, b * D:(b + 1) * D], scbc[:, c, b, :],
                                                wmod[:, c, kind * D:(kind + 1) * D],
                                                start=c == 0, stop=c == DC - 1)
            last.then_inc(gate_mm, 1)

            def transpose_xn(m, n):
                pe.wait_ge(xn_done, m * NT + n * TB + TB)
                for c in range(DC):
                    i = m * NB * DC + n * DC + c
                    if i >= 4:
                        pe.wait_ge(hT_hi, i - 3)
                    for t in range(TB):
                        last = nc.tensor.transpose(four[i % 4][:, t * P:(t + 1) * P],
                                                   xn[:, t, c * P:(c + 1) * P], ident[:, :])
                    last.then_inc(xnT_mm, 1)

            pe.wait_ge(const_done, 2)
            for n in range(NB):
                transpose_xn(0, n)

            def proj_mms(a, b, g):
                w, blk = g // 2, g % 2
                cols = slice(b * S + blk * BANK, b * S + (blk + 1) * BANK)
                return [(st[:, w, c, :], mov[:, c, cols]) for c in range(DC)
                        for st, mov in ((wqkh[a], hTh), (wqkh[a], hTl), (wqkl[a], hTh))]

            def run_proj(n, unit, g, half):
                a, b = UNIT[unit]
                mms = proj_mms(a, b, g)
                if half == 0 and (not isinstance(n, int) or n >= 1):
                    pe.wait_ge(proj_hi, n)
                for m in range(half * 3, half * 3 + 3):
                    last = nc.tensor.matmul(proj[:, :], *mms[m], start=m == 0, stop=m == YM - 1)
                if half:
                    last.then_inc(proj_mm, 1)

            pe.wait_ge(hT_lo, NB * DC)
            pe.wait_ge(wqk_lo, 2)
            for g in range(4):
                for half in range(2):
                    run_proj(g, 0, g, half)

            def run_scores(t, par, buf):
                qt = t % QT
                tile = slice(qt * P, (qt + 1) * P)
                qh, ql, kh, kl = (qk[:, par, i, :] for i in range(4))
                for n, (st, mov) in enumerate(((qh, kh), (qh, kl), (ql, kh))):
                    for h in range(2):
                        last = nc.tensor.matmul(score[buf][:, h, :], st[:, tile],
                                                mov[:, h * BANK:(h + 1) * BANK], start=n == 0, stop=n == 2)
                last.then_inc(score_mm, 1)

            def run_y(n, i, m, b):
                c, part = m // 3, m % 3
                if m == 0 and (not isinstance(n, int) or n + i >= 2):
                    pe.wait_ge(y_scaled, n + i - 1)
                st, mov = ((hTh, mvoh), (hTh, mvol), (hTl, mvoh))[part]
                t = b * QT + i
                last = nc.tensor.matmul(ybank[i % 2][:, :], st[:, c, t * P:(t + 1) * P], mov[:, c, :],
                                        start=m == 0, stop=m == YM - 1)
                if m == YM - 1:
                    last.then_inc(y_mm, 1)

            def run_colsum(p, par, done, what):
                pe.wait_ge(acc_done, done)
                wait_misc(p, what)
                for kt in range(QT):
                    last = nc.tensor.matmul(misc[:, kt:kt + 1], psumw[:, par, kt * P:(kt + 1) * P],
                                            ones[:, 0:1], start=True, stop=True)
                last.then_inc(misc_mm, 1)

            def wait_misc(p, what):
                if what != M_T or not isinstance(p, int) or p > 0:
                    pe.wait_ge(misc_free, misc_n(p, what) - 1)

            def run_wvT(p):
                pe.wait_ge(wqkv_in, p * 48 + 48)
                wait_misc(p, M_T)
                for a in range(2):
                    for c in range(DC):
                        at = (a * DC + c) * P
                        last = nc.tensor.transpose(misc[:, at:at + P], wraw[:, 2, c, a * DH:(a + 1) * DH],
                                                   ident[:, :])
                last.then_inc(misc_mm, 1)

            def run_mvo(p, c, what):
                pe.wait_ge(wo_lo, p + 1)
                wait_misc(p, what)
                for a in range(2):
                    last = three(misc[:, a * D:(a + 1) * D], wvTh[:, a, c, :], wvTl[:, a, c, :],
                                 woh[:, a, :], wol[:, a, :], True, True)
                last.then_inc(misc_mm, 1)

            def run_ffn_transposes(k):
                if k == 0:
                    pe.wait_ge(ffnw_f, GU + DC)
                if k >= 2:
                    pe.wait_ge(ffnw_lo, k - 1)
                bank, dst = ffn_banks[k], ybank[k % 2]
                if bank[0] == "gu":
                    _, c, s, n = bank
                    for i in range(n):
                        last = nc.tensor.transpose(dst[:, i * P:(i + 1) * P],
                                                   wgu_f[:, s + i, c * P:(c + 1) * P], ident[:, :])
                else:
                    _, k0, n, rows = bank
                    for i in range(n):
                        for c in range(DC):
                            last = nc.tensor.transpose(
                                dst[0:rows, i * D + c * P:i * D + (c + 1) * P],
                                wdraw[:, c, (k0 + i) * P:(k0 + i) * P + rows], ident[:, :])
                last.then_inc(ffnw_mm, 1)

            def pair(p, first, last):
                for t in range(STEPS):
                    j, qt = t // QT, t % QT
                    if not (last and j == UNITS - 1):
                        if j == UNITS - 1 and qt == 0:
                            pe.wait_ge(wqk_lo, p * 2 + 3)
                        if j == 0 and qt == 0:
                            pe.wait_ge(wqk_lo, p * 2 + 2)
                        run_proj(p * (4 * UNITS) + 4 * (j + 1) + qt // 2, (j + 1) % UNITS, qt // 2, qt % 2)
                    if qt == 0:
                        pe.wait_ge(proj_lo, p * (4 * UNITS) + 4 * (j + 1))
                    if not (first and t < 2):
                        pe.wait_ge(exp_done, p * STEPS + t - 1)
                    run_scores(t, j % 2, t % 2)
                    if qt == CSTEP and not (first and j == 0):
                        what = (-1, M_C0, M_C1, M_C2)[j]
                        run_colsum(p, (j - 1) % 2, p * STEPS + j * QT, what)
                    if (j, qt) == T_AT:
                        run_wvT(p)
                    if (j, qt) == M0_AT:
                        pe.wait_ge(misc_free, misc_n(p, M_T))
                        run_mvo(p, 0, M_M0)
                    if (j, qt) == M1_AT:
                        run_mvo(p, 1, M_M1)
                    phase = j // 2
                    k = t - phase * 2 * QT - Y0
                    if k >= 0 and not (first and phase == 0):
                        if k == 0:
                            pe.wait_ge(misc_free, misc_n(p, M_C1 if phase else -1))
                        for m in range(PER * k, PER * k + PER):
                            run_y(y_count(p, phase), m // YM, m % YM, 1 - phase)
                    if first and phase == 0 and 0 <= k < len(ffn_banks):
                        run_ffn_transposes(k)

            pair(0, True, False)
            with pe.Fori(1, PAIRS - 1) as p:
                pair(p, False, False)
            pair(PAIRS - 1, False, True)
            run_colsum(PAIRS - 1, (UNITS - 1) % 2, PAIRS * STEPS, M_C3)
            pe.wait_ge(misc_free, misc_n(PAIRS - 1, M_C3))
            for m in range(QT * YM):
                run_y(y_count(PAIRS, 0), m // YM, m % YM, 1)

            def gate_up(nb):
                cols = slice(nb * BANK, (nb + 1) * BANK)
                for k in range(HK):
                    n = nb * HK + k
                    if n >= 2:
                        pe.wait_ge(act_done, n - 1)
                    if k == 1:
                        pe.wait_ge(hT_hi, NB * DC + min(nb | 1, NB - 1) * DC + DC)
                    for half, slot in enumerate((k, HF + k) if k < HF else (2 * HF,)):
                        for c in range(DC):
                            last = three(four[2 * (n % 2) + half], wguh[:, c, slot * P:(slot + 1) * P],
                                         wgul[:, c, slot * P:(slot + 1) * P], hTh[:, c, cols],
                                         hTl[:, c, cols], c == 0, c == DC - 1)
                    last.then_inc(gu_mm, 1)

            def run_down(nb):
                if nb:
                    pe.wait_ge(down_free, TB * nb)
                for ks in (range(HF), range(HF, HK)):
                    for t in range(TB):
                        tile = slice(t * P, (t + 1) * P)
                        for k in ks:
                            rows = P if k < HF else HR
                            if t == 0:
                                pe.wait_ge(act_lo, nb * HK + k + 1)
                            last = three(down[t], acth[0:rows, k, tile], actl[0:rows, k, tile],
                                         wdh[0:rows, k, :], wdl[0:rows, k, :], k == 0, k == HK - 1)
                        if k == HK - 1:
                            last.then_inc(down_mm, 1)

            for half in range(B):
                blocks = range(half * (NB // B), (half + 1) * (NB // B))
                for nb in blocks:
                    transpose_xn(1, nb)
                for nb in blocks:
                    pe.wait_ge(hT_lo, NB * DC + (nb + 1) * DC)
                    gate_up(nb)
                    run_down(nb)

        @block.vector
        def _(dve):
            links = [0]

            def link(ins):
                links[0] += 1
                ins.then_inc(dve_chain, 1)
                dve.wait_ge(dve_chain, links[0])

            dve.wait_ge(siluc_done, 1)
            nc.vector.tensor_copy(scbc, siluc[:, :, :].unsqueeze(3).broadcast_to([P, DC, B, P]))\
              .then_inc(scbc_done, 1)

            def statistics(t):
                link(nc.vector.bn_stats(stats[:, t, :], x[:, t, :]))
                return nc.vector.bn_aggr(mv[:, t, :], stats[:, t, :])

            def add_eps(tiles):
                nc.vector.tensor_scalar_add(mv[:, tiles, 1], mv[:, tiles, 1], EPS).then_inc(stats_done, 1)

            def normalise(m, n):
                if n or m:
                    dve.wait_ge(xnT_mm, (m * NB + n) * DC)
                for t in range(TB):
                    tt = n * TB + t
                    nc.vector.tensor_scalar(xn[:, t, :], x[:, tt, :], mv[:, tt, 0:1], rstd[:, tt:tt + 1],
                                            ALU.subtract, ALU.mult).then_inc(xn_done, 1)

            def split_hT(m, n):
                cols = slice(n * BANK, (n + 1) * BANK)
                for c in range(DC):
                    i = m * NB * DC + n * DC + c
                    dve.wait_ge(hT_hi, i + 1)
                    nc.vector.tensor_tensor(hTl[:, c, cols], htmp[:, i % 2, :], f32(hTh[:, c, cols]),
                                            ALU.subtract).then_inc(hT_lo, 1)

            for n in range(NB):
                dve.wait_ge(x_in[n], 16)
                for t in range(TB):
                    link(statistics(n * TB + t))
            add_eps(slice(0, NT))
            dve.wait_ge(std_done, 1)
            link(nc.vector.reciprocal(rstd[:, :], std[:, :]))
            normalise(0, 0)
            dve.wait_ge(mod_mm, 1)
            mod_ps = misc[:, 0:4 * DC * B].rearrange("p (n c b) -> p n c b", n=4, c=DC)
            for n in range(4):
                last = nc.vector.tensor_scalar_add(modc[:, n, :, :], mod_ps[:, n, :, :], float(n % 2))
                if n < 3:
                    link(last)
            last.then_inc(mod_done, 1)
            for n in range(1, NB):
                normalise(0, n)
                split_hT(0, n - 1)
            split_hT(0, NB - 1)
            dve.wait_ge(gate_mm, 1)
            for n in range(2):
                g = ybank[n][:, :].rearrange("p (b d) -> p b d", b=B)
                link(nc.vector.tensor_copy(gtmp[:, n, :, :], g))
                link(nc.vector.scalar_tensor_tensor(gates[:, n, :, :], gtmp[:, n, :, :], -1.0,
                                                    gtmp[:, n, :, :], ALU.mult, ALU.max))
                link(nc.vector.tensor_scalar_max(gates[:, n, :, :], gates[:, n, :, :], GATE_MIN))
                link(nc.vector.tensor_scalar(gtmp[:, n, :, :], gtmp[:, n, :, :], 0.0, 2.0,
                                             ALU.is_ge, ALU.mult))
                link(nc.vector.scalar_tensor_tensor(gates[:, n, :, :], gtmp[:, n, :, :], -1.0,
                                                    gates[:, n, :, :], ALU.add, ALU.mult))

            def run_max(p, t):
                dve.wait_ge(score_mm, p * STEPS + t + 1)
                nc.vector.tensor_reduce(nmax[:, t % 4:t % 4 + 1], score[t % 2][:, :, :], AX.XY, ALU.max,
                                        negate=True).then_inc(max_done, 1)

            def run_acc(p, t):
                s, par, buf = t % STEPS, (t % STEPS) // QT % 2, t % 4
                dve.wait_ge(rz_done, p * STEPS + t + 1)
                if s % QT == 0:
                    last = nc.vector.tensor_scalar_mul(psumw[:, par, :], prob[:, buf, :], rz[:, buf:buf + 1])
                else:
                    dve.wait_ge(acc_done, p * STEPS + t)
                    last = nc.vector.scalar_tensor_tensor(psumw[:, par, :], prob[:, buf, :],
                                                          rz[:, buf:buf + 1], psumw[:, par, :],
                                                          ALU.mult, ALU.add)
                last.then_inc(acc_done, 1)

            def run_rz(p, t):
                dve.wait_ge(exp_done, p * STEPS + t + 1)
                nc.vector.reciprocal(rz[:, t % 4:t % 4 + 1], zsum[:, t % 4:t % 4 + 1]).then_inc(rz_done, 1)

            def colsum_out(p, what, unit):
                dve.wait_ge(misc_mm, misc_n(p, what))
                nc.vector.tensor_copy(colsum[:, unit, :], misc[:, 0:QT]).then_inc(misc_free, 1)

            def misc_lo(n, lo, hi):
                dve.wait_ge(misc_hi, n + 1)
                nc.vector.tensor_tensor(lo, misc[:, :], f32(hi), ALU.subtract).then_inc(misc_free, 1)

            def pair(p, first, last):
                for t in range(STEPS):
                    j, qt = t // QT, t % QT
                    run_max(p, t)
                    if qt == CSTEP and not (first and j == 0):
                        pass
                    if (j, qt) == T_EV:
                        misc_lo(p * 3, flat(wvTl), flat(wvTh))
                    if (j, qt) == M0_EV:
                        misc_lo(p * 3 + 1, mvol[:, 0, :], mvoh[:, 0, :])
                    if (j, qt) == M1_EV:
                        misc_lo(p * 3 + 2, mvol[:, 1, :], mvoh[:, 1, :])
                    k = t - 1 - Y0
                    if first and 0 <= k < len(ffn_banks):
                        rows, cols, hi, lo = ffn_views(ffn_banks[k])
                        dve.wait_ge(ffnw_hi, k + 1)
                        nc.vector.tensor_tensor(lo, ybank[k % 2][0:rows, 0:cols], f32(hi), ALU.subtract)\
                          .then_inc(ffnw_lo, 1)
                    if not (first and t < 2):
                        run_acc(p, t - 2)
                    if not (first and t < 1):
                        run_rz(p, t - 1)
                    if qt == CSTEP and not (first and j == 0):
                        colsum_out(p, (-1, M_C0, M_C1, M_C2)[j], (j - 1) % UNITS)

            def flat(ap):
                return ap[:, :, :, :].rearrange("p a c n -> p (a c n)")

            pair(0, True, False)
            with dve.Fori(1, PAIRS - 1) as p:
                pair(p, False, False)
            pair(PAIRS - 1, False, True)
            run_acc(PAIRS, -2)
            run_rz(PAIRS, -1)
            run_acc(PAIRS, -1)
            colsum_out(PAIRS - 1, M_C3, UNITS - 1)

            def residual(b):
                for i in range(QT):
                    t = b * QT + i
                    dve.wait_ge(y_added, (y_count(PAIRS - 1 + b, 1 - b) + i + 1) * 2)
                    link(nc.vector.tensor_tensor(attn[:, t, :], attn[:, t, :], gates[:, 0, b, :], ALU.mult))
                    link(nc.vector.tensor_tensor(x[:, t, :], x[:, t, :], attn[:, t, :], ALU.add))
                    link(statistics(t))
                add_eps(slice(b * QT, (b + 1) * QT))
                dve.wait_ge(std_done, 2 + b)
                link(nc.vector.reciprocal(rstd[:, b * QT:(b + 1) * QT], std[:, b * QT:(b + 1) * QT]))

            def ffn_mult(n):
                k = n % HK
                rows = P if k < HF else HR
                up = four[2 * (n % 2) + 1] if k < HF else four[2 * (n % 2)][HR:2 * HR, :]
                dve.wait_ge(sil_done, n + 1)
                if n >= 2:
                    dve.wait_ge(act_lo, n - 1)
                nc.vector.tensor_tensor(act32[0:rows, n % 2, :], up[0:rows, :], silg[0:rows, n % 2, :],
                                        ALU.mult).then_inc(act_done, 1)

            def finish(nb):
                for i in range(TB):
                    t = nb * TB + i
                    dve.wait_ge(down_mm, t + 1)
                    nc.vector.tensor_tensor(attn[:, t, :], down[i], gates[:, 1, t // QT, :], ALU.mult)\
                      .then_inc(down_free, 1)
                    dve.wait_ge(down_free, t + 1)
                    nc.vector.tensor_tensor(attn[:, t, :], attn[:, t, :], x[:, t, :], ALU.add)\
                      .then_inc(out_done, 1)

            for half in range(B):
                residual(half)
                blocks = range(half * (NB // B), (half + 1) * (NB // B))
                for nb in blocks:
                    normalise(1, nb)
                    split_hT(1, nb)
                for nb in blocks:
                    for k in range(HK):
                        ffn_mult(nb * HK + k)
                    finish(nb)


_INS = ["L0_attn_x", "L0_attn_w_qkv", "L0_attn_w_o", "L0_ffn_wq_gate", "L0_ffn_s_gate", "L0_ffn_wq_up",
        "L0_ffn_s_up", "L0_ffn_wq_down", "L0_ffn_s_down", "L0_c", "L0_wmod"]


def kernel(**inputs):
    import numpy as np
    import concourse.bacc as bacc
    from concourse.bass_utils import run_bass_kernel_spmd

    nc = bacc.Bacc("TRN2", target_bir_lowering=False, num_devices=1)
    arrays, args = {}, []
    for name in _INS:
        a = np.ascontiguousarray(inputs[name])
        arrays[f"in_{name}"] = a
        args.append(nc.dram_tensor(f"in_{name}", a.shape, mybir.dt.from_np(a.dtype), kind="ExternalInput").ap())
    x = inputs["L0_attn_x"]
    args.append(nc.dram_tensor("out", x.shape, F32, kind="ExternalOutput").ap())
    adaln_block(nc, *args)
    r = run_bass_kernel_spmd(nc, [arrays], core_ids=[0])
    return r.results[0]["out"]
```

```python
from contextlib import ExitStack

import concourse.bass as bass
from concourse import mybir

F32 = mybir.dt.float32
F32R = mybir.dt.float32r
I32 = mybir.dt.int32
ALU = mybir.AluOpType
ACT = mybir.ActivationFunctionType
AX = mybir.AxisListType

P = 128
BANK = 512
EPS = 1e-5
ZERO_POINT = 128.0
GATE_MIN = 0.25


def adaln_block(nc, x_d, w_qkv_d, w_o_d, wq_gate_d, s_gate_d, wq_up_d, s_up_d, wq_down_d, s_down_d,
                c_d, wmod_d, out_d):
    B, S, D = x_d.shape
    DH = 128
    NH = w_o_d.shape[0] // DH
    HID = wq_gate_d.shape[0]
    SCALE = float(DH) ** -0.5
    DC = D // P
    QT = S // P
    NT = B * QT
    PAIRS = NH // 2
    UNITS = 2 * B
    STEPS = UNITS * QT
    HF = HID // P
    HR = HID - HF * P
    HK = HF + 1
    GU = 2 * HF + 1
    TB = BANK // P
    NB = NT // TB
    assert B == 2 and D == 256 and S == 1024 and NH % 2 == 0 and HR == 64

    UNIT = [(0, 0), (1, 0), (0, 1), (1, 1)]
    CSTEP = 3
    T_AT, M0_AT, M1_AT = 5, 12, 14
    T_EV, M0_EV, M1_EV = 6, 13, 15
    WO_AT, WQK_AT = 8, (2 * QT + 2, 3 * QT + 2)

    YM = 3 * DC
    YRANGE = [(0, M0_AT), (M1_EV, STEPS - 1)]
    YSUM = [CSTEP, 2 * QT + CSTEP]

    def y_schedule(phase):
        t0, t1 = YRANGE[phase]
        other = {t: 8 for t in range(CSTEP, STEPS, QT)}
        other.update({T_AT: 2, M0_AT: 6})
        done = {t0 - 1: 0}
        for t in range(t0, t1 + 1):
            load = QT * YM - done[t - 1] + sum(other.get(u, 0) for u in range(t, t1 + 1))
            n = max(0, -(-load // (t1 - t + 1)) - other.get(t, 0))
            limit = 3 if t == M1_EV else 2 * YM if t <= YSUM[phase] + 1 else QT * YM
            done[t] = min(done[t - 1] + n, limit) if t < t1 else QT * YM
        return done

    YDONE = [y_schedule(phase) for phase in range(2)]

    def y_matmuls(t):
        for phase, (t0, t1) in enumerate(YRANGE):
            if t0 <= t <= t1:
                return phase, range(YDONE[phase][t - 1], YDONE[phase][t])
        return 0, range(0)

    def y_scales(t):
        tiles = []
        for phase in range(2):
            for i in range(QT):
                done = min(u for u, n in YDONE[phase].items() if n >= (i + 1) * YM)
                if t == max(done + 1, YSUM[phase]):
                    tiles.append((phase, i))
        return tiles

    assert y_scales(STEPS) == [(1, QT - 1)]

    ctx = ExitStack()
    with ctx:
        def sb(name, shape, dt=F32):
            return ctx.enter_context(nc.sbuf_tensor(name, shape, dt))

        def pb(name, shape):
            return ctx.enter_context(nc.psum_tensor(name, shape, F32))

        def sem(name):
            return ctx.enter_context(nc.semaphore(name))

        x = sb("x", [P, NT, D])
        hTh = sb("hTh", [P, DC, B * S], F32R)
        hTl = sb("hTl", [P, DC, B * S], F32R)
        attn = sb("attn", [P, NT, D])
        qk = sb("qk", [P, 2, 4, S], F32R)
        prob = sb("prob", [P, 4, S])
        psumw = sb("psumw", [P, 2, S])
        praw = sb("praw", [P, 2, BANK])
        ysc = sb("ysc", [P, 2, 2 * D])
        wraw = sb("wraw", [P, 3, DC, 2 * DH])
        woraw = sb("woraw", [P, 2, D])
        wqkh = [sb(f"wqkh{a}", [P, 2, DC, DH], F32R) for a in range(2)]
        wqkl = [sb(f"wqkl{a}", [P, 2, DC, DH], F32R) for a in range(2)]
        woh = sb("woh", [P, 2, D], F32R)
        wol = sb("wol", [P, 2, D], F32R)
        wvTh = sb("wvTh", [P, 2, DC, P], F32R)
        wvTl = sb("wvTl", [P, 2, DC, P], F32R)
        mvoh = sb("mvoh", [P, DC, 2 * D], F32R)
        mvol = sb("mvol", [P, DC, 2 * D], F32R)
        wguh = sb("wguh", [P, DC, GU * P], F32R)
        wgul = sb("wgul", [P, DC, GU * P], F32R)
        wdh = sb("wdh", [P, HK, D], F32R)
        wdl = sb("wdl", [P, HK, D], F32R)
        wdraw = sb("wdraw", [P, DC, HID])
        ident = sb("ident", [P, P])
        ones = sb("ones", [P, 2])
        gates = sb("gates", [P, 2, B, D])
        modc = sb("modc", [P, 4, DC, B])
        cT = sb("cT", [P, DC, B])
        siluc = sb("siluc", [P, DC, B])
        sgu = sb("sgu", [P, GU])
        sdn = sb("sdn", [P, DC])
        stats = sb("stats", [P, NT, 6])
        mv = sb("mv", [P, NT, 2])
        minus_half = sb("minus_half", [P, TB])
        rstd = sb("rstd", [P, NT])
        nmax = sb("nmax", [P, 4])
        zsum = sb("zsum", [P, 4])
        rz = sb("rz", [P, 4])
        colsum = sb("colsum", [P, UNITS, QT])

        wmod = prob[:, 0:3, :].rearrange("p a n -> p (a n)").rearrange("p (c n) -> p c n", c=DC)
        htmp = prob[:, 3, :].rearrange("p (a n) -> p a n", a=2)
        xn_praw, xn_ysc = (m[:, :, :].rearrange("p a n -> p (a n)").rearrange("p (t d) -> p t d", t=TB)
                           for m in (praw, ysc))
        scbc = psumw[:, 0, 0:DC * B * P].rearrange("p (c b n) -> p c b n", c=DC, b=B)
        gtmp = psumw[:, 1, :].rearrange("p (g b d) -> p g b d", g=2, b=B)
        wgu_f = attn[:, 0:GU, :]
        wgu_i = attn[:, 0:GU, :].bitcast(I32)
        wd_i = wdraw[:, :, :].bitcast(I32)
        acth = qk[:, 0, 0:3, :].rearrange("p a n -> p (a n)").rearrange("p (k n) -> p k n", k=HK)
        actl = qk[:, 1, 0:3, :].rearrange("p a n -> p (a n)").rearrange("p (k n) -> p k n", k=HK)
        silg = prob[:, 0, :].rearrange("p (a n) -> p a n", a=2)
        act32 = prob[:, 1, :].rearrange("p (a n) -> p a n", a=2)

        score = [pb(f"score{i}", [P, 2, BANK]) for i in range(2)]
        proj = pb("proj", [P, BANK])
        misc = pb("misc", [P, BANK])
        ybank = [pb(f"ybank{i}", [P, BANK]) for i in range(2)]
        ylast = [ybank[0], ybank[1], proj, score[0][:, 0, :], score[0][:, 1, :], score[1][:, 0, :],
                 score[1][:, 1, :], ybank[0]]
        four = [score[0][:, 0, :], score[0][:, 1, :], score[1][:, 0, :], score[1][:, 1, :]]
        down = [ybank[0][:, 0:D], ybank[1][:, 0:D], proj[:, 0:D], misc[:, 0:D]]

        x_in = [sem(f"x_in{i}") for i in range(NB)]
        c_in, ffnw_in = sem("c_in"), sem("ffnw_in")
        wmod_in = [sem(f"wmod_in{m}") for m in range(2)] + [sem("wmodg_in")]
        wqkv_in, wo_in = sem("wqkv_in"), sem("wo_in")
        stored = sem("stored")
        const_done, pool_chain, dve_chain = sem("const_done"), sem("pool_chain"), sem("dve_chain")
        siluc_done, scbc_done, mod_mm, gate_mm, gate_read, mod_done = (sem(n) for n in (
            "siluc_done", "scbc_done", "mod_mm", "gate_mm", "gate_read", "mod_done"))
        stats_done, rstd_done, xn_done = sem("stats_done"), sem("rstd_done"), sem("xn_done")
        xnT_mm, hT_hi, hT_lo = sem("xnT_mm"), sem("hT_hi"), sem("hT_lo")
        wqk_hi, wqk_lo, wo_hi, wo_lo = sem("wqk_hi"), sem("wqk_lo"), sem("wo_hi"), sem("wo_lo")
        proj_mm, proj_read, proj_hi, first_lo, proj_lo = (sem(n) for n in (
            "proj_mm", "proj_read", "proj_hi", "first_lo", "proj_lo"))
        score_mm, max_done, exp_done, rz_done, acc_done = (sem(n) for n in (
            "score_mm", "max_done", "exp_done", "rz_done", "acc_done"))
        misc_mm, misc_hi, misc_free = sem("misc_mm"), sem("misc_hi"), sem("misc_free")
        y_mm, y_scaled, y_added = sem("y_mm"), sem("y_scaled"), sem("y_added")
        ffnw_f, ffnw_mm, ffnw_hi, ffnw_lo, attn_zero = (sem(n) for n in (
            "ffnw_f", "ffnw_mm", "ffnw_hi", "ffnw_lo", "attn_zero"))
        gu_mm, sil_done, act_done, act_hi, act_lo = (sem(n) for n in (
            "gu_mm", "sil_done", "act_done", "act_hi", "act_lo"))
        down_mm, down_free, out_done = sem("down_mm"), sem("down_free"), sem("out_done")

        def f32(ap):
            return ap.bitcast(F32)

        def y_count(p, phase):
            return p * 2 * QT + (0 if phase else -QT)

        MISC = 7
        M_T, M_C0, M_M0, M_M1, M_C1, M_C2, M_C3 = range(MISC)

        def xn_of(m, n):
            return xn_ysc if m == 0 and n else xn_praw

        def xnT_bank(m, n, c):
            return four[(n * DC + c) % 4] if m == 0 else four[c]

        def misc_n(p, what):
            return p * MISC + what + 1

        def proj_at(t):
            return (t + 1) // QT + 1, (t + 1) % QT // 2, (t + 1) % 2

        ffn_banks = [("gu", c, s, min(4, GU - s)) for c in range(DC) for s in range(0, GU, 4)]
        ffn_banks += [("dn", k, min(2, HF - k), P) for k in range(0, HF, 2)] + [("dn", HF, 1, HR)]
        FFN_AT = 1
        assert FFN_AT + len(ffn_banks) < YRANGE[0][1]

        def ffn_views(bank):
            if bank[0] == "gu":
                _, c, s, n = bank
                return P, n * P, wguh[:, c, s * P:(s + n) * P], wgul[:, c, s * P:(s + n) * P]
            _, k, n, rows = bank
            return (rows, n * D, wdh[0:rows, k:k + n, :].rearrange("p k d -> p (k d)"),
                    wdl[0:rows, k:k + n, :].rearrange("p k d -> p (k d)"))

        qkv_v = w_qkv_d.rearrange("(c p) (w n) -> w p c n", p=P, w=3)
        wo_v = w_o_d.rearrange("(h d) n -> d h n", d=DH)
        x_v = x_d.rearrange("b (t p) d -> p (b t) d", p=P)
        out_v = out_d.rearrange("b (t p) d -> p (b t) d", p=P)

        block = ctx.enter_context(nc.Block())

        @block.sync
        def _(sp):
            def load_qkv(p):
                for w in range(3):
                    sp.dma_start(wraw[:, w, :, :], qkv_v[w, :, :, bass.ds(p * (2 * DH), 2 * DH)])\
                      .then_inc(wqkv_in, 16)

            def load_wo(p):
                sp.dma_start(woraw[:, :, :], wo_v[:, bass.ds(p * 2, 2), :]).then_inc(wo_in, 16)

            def load_x(n):
                sp.dma_start(x[:, n * TB:(n + 1) * TB, :], x_v[:, n * TB:(n + 1) * TB, :])\
                  .then_inc(x_in[n], 16)

            def load_wmod(kind, n, signal):
                cols = slice(kind * D, (kind + n) * D)
                sp.dma_start(wmod[:, :, cols], wmod_v[:, :, cols]).then_inc(signal, 16)

            wmod_v = wmod_d.rearrange("(c p) n -> p c n", p=P)
            load_x(0)
            with nc.allow_non_contiguous_dma(reason="a few hundred words, once"):
                for c in range(DC):
                    sp.dma_start(cT[:, c, :], c_d[:, c * P:(c + 1) * P].rearrange("b p -> p b"))\
                      .then_inc(c_in, 16)
            load_wmod(0, 2, wmod_in[0])
            load_x(1)
            load_qkv(0)
            load_wmod(3, 2, wmod_in[1])
            for kind in (2, 5):
                load_wmod(kind, 1, wmod_in[2])
            load_x(2)
            load_x(3)
            load_wo(0)
            for n, (w_d, s_d) in enumerate(((wq_gate_d, s_gate_d), (wq_up_d, s_up_d))):
                rem = slice(n * HR, (n + 1) * HR)
                sp.dma_start(wgu_i[:, n * HF:(n + 1) * HF, :],
                             w_d[0:HF * P, :].rearrange("(k p) d -> p k d", p=P)).then_inc(ffnw_in, 16)
                sp.dma_start(wgu_i[rem, 2 * HF, :], w_d[HF * P:HID, :]).then_inc(ffnw_in, 16)
                with nc.allow_non_contiguous_dma(reason="one scale per row"):
                    sp.dma_start(sgu[:, n * HF:(n + 1) * HF],
                                 s_d[0:HF * P].rearrange("(k p) -> p k", p=P)).then_inc(ffnw_in, 16)
                    sp.dma_start(sgu[rem, 2 * HF:GU],
                                 s_d[HF * P:HID].rearrange("(p a) -> p a", a=1)).then_inc(ffnw_in, 16)
            sp.dma_start(wd_i, wq_down_d.rearrange("(c p) k -> p c k", p=P)).then_inc(ffnw_in, 16)
            with nc.allow_non_contiguous_dma(reason="one scale per row"):
                sp.dma_start(sdn[:, :], s_down_d.rearrange("(c p) -> p c", p=P)).then_inc(ffnw_in, 16)

            def next_pair(p):
                sp.wait_ge(misc_mm, misc_n(p, M_T))
                sp.wait_ge(wqk_lo, p * 2 + 2)
                load_qkv(p + 1)
                sp.wait_ge(wo_lo, p + 1)
                load_wo(p + 1)

            with sp.Fori(0, PAIRS - 1) as p:
                next_pair(p)
            for t in range(NT):
                sp.wait_ge(out_done, t + 1)
                sp.dma_start(out_v[:, t, :], attn[:, t, :]).then_inc(stored, 16)
            sp.wait_ge(stored, 16 * NT)

        @block.gpsimd
        def _(pool):
            nc.gpsimd.memset(ident[:, :], 0.0).then_inc(pool_chain, 1)
            nc.gpsimd.memset(ones[:, :], 1.0).then_inc(const_done, 1)
            nc.gpsimd.memset(minus_half[:, :], -0.5).then_inc(pool_chain, 1)
            pool.wait_ge(pool_chain, 2)
            nc.gpsimd.affine_select(out=ident[:, :], in_=ident[:, :], compare_op=ALU.not_equal, fill=1.0,
                                    base=0, pattern=[[-1, P]], channel_multiplier=1).then_inc(const_done, 1)

            def split_wqk(p, a):
                pool.wait_ge(wqk_hi, p * 2 + a + 1)
                nc.gpsimd.tensor_tensor(wqkl[a][:, :, :, :], wraw[:, 0:2, :, a * DH:(a + 1) * DH],
                                        f32(wqkh[a][:, :, :, :]), ALU.subtract).then_inc(wqk_lo, 1)

            def split_wo(p):
                pool.wait_ge(wo_hi, p + 1)
                nc.gpsimd.tensor_tensor(wol[:, :, :], woraw[:, :, :], f32(woh[:, :, :]),
                                        ALU.subtract).then_inc(wo_lo, 1)

            def proj_split(n, par, g):
                w, blk = g // 2, g % 2
                cols = slice(blk * BANK, (blk + 1) * BANK)
                pool.wait_ge(proj_hi, n + 1)
                nc.gpsimd.tensor_tensor(qk[:, par, 2 * w + 1, cols], praw[:, g % 2, :],
                                        f32(qk[:, par, 2 * w, cols]), ALU.subtract).then_inc(proj_lo, 1)

            def y_add(n, i, b):
                t = b * QT + i
                pool.wait_ge(y_scaled, n + 1)
                if i == 0:
                    pool.wait_ge(attn_zero, 1)
                for a in range(2):
                    if a:
                        pool.wait_ge(y_added, n * 2 + 1)
                    nc.gpsimd.tensor_tensor(attn[:, t, :], attn[:, t, :], ysc[:, i % 2, a * D:(a + 1) * D],
                                            ALU.add).then_inc(y_added, 1)

            def rstd_block(m, n):
                tiles = slice(n * TB, (n + 1) * TB)
                pool.wait_ge(stats_done, m * NB + n + 1)
                nc.gpsimd.tensor_tensor(rstd[:, tiles], mv[:, tiles, 1], minus_half[:, :], ALU.pow)\
                  .then_inc(rstd_done, 1)

            rstd_block(0, 0)
            rstd_block(0, 1)
            for a in range(2):
                split_wqk(0, a)
            rstd_block(0, 2)
            rstd_block(0, 3)
            pool.wait_ge(ffnw_in, 10 * 16)
            for s in range(GU):
                nc.gpsimd.tensor_scalar(wgu_f[:, s, :], wgu_i[:, s, :], -ZERO_POINT, sgu[:, s:s + 1],
                                        ALU.add, ALU.mult).then_inc(ffnw_f, 1)
            for c in range(DC):
                nc.gpsimd.tensor_scalar(wdraw[:, c, :], wd_i[:, c, :], -ZERO_POINT, sdn[:, c:c + 1],
                                        ALU.add, ALU.mult).then_inc(ffnw_f, 1)

            def pair(p, first, last):
                for t in range(STEPS):
                    ahead, g, half = proj_at(t)
                    if half and not (last and ahead >= UNITS):
                        proj_split(p * (4 * UNITS) + 4 * ahead + g, ahead % 2, g)
                    if t == WO_AT:
                        split_wo(p)
                    if t in WQK_AT and not last:
                        split_wqk(p + 1, WQK_AT.index(t))
                    if first and t == YRANGE[1][0]:
                        pool.wait_ge(ffnw_mm, len(ffn_banks))
                        nc.gpsimd.memset(attn[:, :, :], 0.0).then_inc(attn_zero, 1)
                    if t == 0 and not first:
                        y_add(y_count(p, 0) - 1, QT - 1, 0)
                    for phase, tile in y_scales(t):
                        if not (first and phase == 0):
                            y_add(y_count(p, phase) + tile, tile, 1 - phase)

            pair(0, True, False)
            with pool.Fori(1, PAIRS - 1) as p:
                pair(p, False, False)
            pair(PAIRS - 1, False, True)
            y_add(y_count(PAIRS, 0) - 1, QT - 1, 0)
            for i in range(QT):
                y_add(y_count(PAIRS, 0) + i, i, 1)
                if i in (2, 5):
                    rstd_block(1, i // 3)
            for n in range(NB * HK):
                k = n % HK
                rows = P if k < HF else HR
                pool.wait_ge(act_hi, n + 1)
                nc.gpsimd.tensor_tensor(actl[0:rows, k, :], act32[0:rows, n % 2, :],
                                        f32(acth[0:rows, k, :]), ALU.subtract).then_inc(act_lo, 1)
                if k == HK - 1 and n // HK + 2 < NB:
                    rstd_block(1, n // HK + 2)

        @block.scalar
        def _(act):
            act.wait_ge(c_in, 16 * DC)
            nc.scalar.activation(siluc[:, :, :], cT[:, :, :], ACT.Silu).then_inc(siluc_done, 1)

            def split_wqk(p, a):
                act.wait_ge(wqkv_in, p * 48 + 48)
                nc.scalar.activation(wqkh[a][:, :, :, :], wraw[:, 0:2, :, a * DH:(a + 1) * DH], ACT.Copy)\
                  .then_inc(wqk_hi, 1)

            def hT_block(m, n, c):
                i = m * NB * DC + n * DC + c
                b = n // (NB // B)
                cols = slice(n * BANK, (n + 1) * BANK)
                act.wait_ge(mod_done, m + 1)
                act.wait_ge(xnT_mm, i + 1)
                if i >= 2:
                    act.wait_ge(hT_lo, i - 1)
                for dst in (htmp[:, i % 2, :], hTh[:, c, cols]):
                    last = nc.scalar.activation(dst, xnT_bank(m, n, c), ACT.Identity,
                                                bias=modc[:, 2 * m, c, b:b + 1],
                                                scale=modc[:, 2 * m + 1, c, b:b + 1])
                last.then_inc(hT_hi, 1)

            def proj_out(n, par, g, bank=proj):
                w, blk = g // 2, g % 2
                act.wait_ge(proj_mm, n + 1)
                if not isinstance(n, int) or n >= 6:
                    act.wait_ge(proj_lo, n - 5)
                elif n >= 2:
                    act.wait_ge(first_lo, n - 1)
                nc.scalar.activation(praw[:, g % 2, :], bank[:, :], ACT.Copy, scale=1.0 if w else SCALE)\
                  .then_inc(proj_read, 1)
                act.wait_ge(proj_read, n + 1)
                nc.scalar.activation(qk[:, par, 2 * w, blk * BANK:(blk + 1) * BANK], praw[:, g % 2, :],
                                     ACT.Copy).then_inc(proj_hi, 1)

            def hT_blocks(m, n):
                for c in range(DC):
                    hT_block(m, n, c)

            hT_blocks(0, 0)
            for a in range(2):
                split_wqk(0, a)
            hT_blocks(0, 1)
            act.wait_ge(gate_mm, 1)
            for n in range(2):
                nc.scalar.activation(gtmp[:, n, :, :], ybank[n][:, :], ACT.Copy).then_inc(gate_read, 1)
            for g in range(4):
                proj_out(g, 0, g, (proj, misc)[g % 2])
                if g + 2 < NB:
                    hT_blocks(0, g + 2)

            def y_scale(n, i, b, sums, bank=None):
                act.wait_ge(y_mm, n + 1)
                if i == 0:
                    act.wait_ge(misc_free, sums)
                if not isinstance(n, int) or n >= 2:
                    act.wait_ge(y_added, n * 2 - 2)
                bank = ybank[i % 2] if bank is None else bank
                for a in range(2):
                    last = nc.scalar.activation(ysc[:, i % 2, a * D:(a + 1) * D],
                                                bank[:, a * D:(a + 1) * D], ACT.Copy,
                                                scale=colsum[:, 2 * b + a, i:i + 1])
                last.then_inc(y_scaled, 1)

            def pair(p, first, last):
                for t in range(STEPS):
                    ahead, g, half = proj_at(t)
                    if half and not (last and ahead >= UNITS):
                        proj_out(p * (4 * UNITS) + 4 * ahead + g, ahead % 2, g)
                    if t == 0 and not first:
                        y_scale(y_count(p, 0) - 1, QT - 1, 0, None)
                    for phase, tile in y_scales(t):
                        if not (first and phase == 0):
                            y_scale(y_count(p, phase) + tile, tile, 1 - phase,
                                    misc_n(p, M_C1 if phase else -1))
                    k = t - 1 - FFN_AT
                    if first and 0 <= k < len(ffn_banks):
                        rows, cols, hi, _ = ffn_views(ffn_banks[k])
                        act.wait_ge(ffnw_mm, k + 1)
                        nc.scalar.activation(hi, ybank[k % 2][0:rows, 0:cols], ACT.Copy)\
                          .then_inc(ffnw_hi, 1)
                    if t == T_EV:
                        act.wait_ge(misc_mm, misc_n(p, M_T))
                        nc.scalar.activation(wvTh[:, :, :, :], misc[:, :], ACT.Copy).then_inc(misc_hi, 1)
                    if t == WO_AT:
                        act.wait_ge(wo_in, p * 16 + 16)
                        nc.scalar.activation(woh[:, :, :], woraw[:, :, :], ACT.Copy).then_inc(wo_hi, 1)
                    for c, at, what in ((0, M0_EV, M_M0), (1, M1_EV, M_M1)):
                        if t == at:
                            act.wait_ge(misc_mm, misc_n(p, what))
                            nc.scalar.activation(mvoh[:, c, :], misc[:, :], ACT.Copy).then_inc(misc_hi, 1)
                    if t in WQK_AT and not last:
                        split_wqk(p + 1, WQK_AT.index(t))
                    act.wait_ge(max_done, p * STEPS + t + 1)
                    if not (first and t < 4):
                        act.wait_ge(acc_done, p * STEPS + t - 3)
                    nc.scalar.activation(prob[:, t % 4, :], score[t % 2][:, :, :], ACT.Exp,
                                         bias=nmax[:, t % 4:t % 4 + 1], scale=1.0,
                                         accum_out=zsum[:, t % 4:t % 4 + 1]).then_inc(exp_done, 1)

            pair(0, True, False)
            with act.Fori(1, PAIRS - 1) as p:
                pair(p, False, False)
            pair(PAIRS - 1, False, True)
            y_scale(y_count(PAIRS, 0) - 1, QT - 1, 0, None)
            for i in range(QT):
                y_scale(y_count(PAIRS, 0) + i, i, 1, misc_n(PAIRS, -1), ylast[i])

            def ffn_act(n):
                k = n % HK
                rows = P if k < HF else HR
                act.wait_ge(gu_mm, n + 1)
                if n >= 2:
                    act.wait_ge(act_done, n - 1)
                nc.scalar.activation(silg[0:rows, n % 2, :], four[2 * (n % 2)][0:rows, :], ACT.Silu)\
                  .then_inc(sil_done, 1)

            def ffn_hi(n):
                k = n % HK
                rows = P if k < HF else HR
                act.wait_ge(act_done, n + 1)
                nc.scalar.activation(acth[0:rows, k, :], act32[0:rows, n % 2, :], ACT.Copy)\
                  .then_inc(act_hi, 1)

            for nb in range(NB):
                hT_blocks(1, nb)
                for k in range(HK):
                    ffn_act(nb * HK + k)
                    if k:
                        ffn_hi(nb * HK + k - 1)
                ffn_hi(nb * HK + HK - 1)

        @block.tensor
        def _(pe):
            def three(out, stat_hi, stat_lo, mov_hi, mov_lo, start, stop):
                nc.tensor.matmul(out, stat_hi, mov_hi, start=start, stop=False)
                nc.tensor.matmul(out, stat_hi, mov_lo, start=False, stop=False)
                return nc.tensor.matmul(out, stat_lo, mov_hi, start=False, stop=stop)

            def modulation(m):
                pe.wait_ge(wmod_in[m], 16)
                if m:
                    pe.wait_ge(mod_done, 1)
                for n, kind in enumerate((3 * m, 3 * m + 1)):
                    for c2 in range(DC):
                        at = (n * DC + c2) * B
                        for c in range(DC):
                            last = nc.tensor.matmul(misc[:, at:at + B],
                                                    wmod[:, c, kind * D + c2 * P:kind * D + (c2 + 1) * P],
                                                    siluc[:, c, :], start=c == 0, stop=c == DC - 1)
                last.then_inc(mod_mm, 1)

            def gate_rows():
                pe.wait_ge(scbc_done, 1)
                pe.wait_ge(wmod_in[2], 32)
                for n, kind in enumerate((2, 5)):
                    for b in range(B):
                        for c in range(DC):
                            last = nc.tensor.matmul(ybank[n][:, b * D:(b + 1) * D], scbc[:, c, b, :],
                                                    wmod[:, c, kind * D:(kind + 1) * D],
                                                    start=c == 0, stop=c == DC - 1)
                last.then_inc(gate_mm, 1)

            def transpose_xn(m, n):
                pe.wait_ge(xn_done, m * NT + n * TB + TB)
                if m == 0 and n >= 2:
                    pe.wait_ge(hT_hi, (n - 1) * DC)
                if m == 1 and n >= 1:
                    pe.wait_ge(act_done, n * HK - 1)
                for c in range(DC):
                    for t in range(TB):
                        last = nc.tensor.transpose(xnT_bank(m, n, c)[:, t * P:(t + 1) * P],
                                                   xn_of(m, n)[:, t, c * P:(c + 1) * P], ident[:, :])
                    last.then_inc(xnT_mm, 1)

            def proj_mms(a, b, g):
                w, blk = g // 2, g % 2
                cols = slice(b * S + blk * BANK, b * S + (blk + 1) * BANK)
                return [(st[:, w, c, :], mov[:, c, cols]) for c in range(DC)
                        for st, mov in ((wqkh[a], hTh), (wqkh[a], hTl), (wqkl[a], hTh))]

            def run_proj(n, unit, g, half, bank=proj, read=None):
                a, b = UNIT[unit]
                mms = proj_mms(a, b, g)
                if half == 0 and read != 0:
                    pe.wait_ge(proj_read, n if read is None else read)
                for m in range(half * 3, half * 3 + 3):
                    last = nc.tensor.matmul(bank[:, :], *mms[m], start=m == 0, stop=m == YM - 1)
                if half:
                    last.then_inc(proj_mm, 1)

            pe.wait_ge(siluc_done, 1)
            modulation(0)
            pe.wait_ge(const_done, 2)
            transpose_xn(0, 0)
            transpose_xn(0, 1)
            modulation(1)
            gate_rows()
            pe.wait_ge(wqk_lo, 2)
            for g in range(4):
                if g < 2:
                    pe.wait_ge(hT_lo, (g + 1) * DC)
                if g == 1:
                    pe.wait_ge(mod_done, 2)
                for half in range(2):
                    run_proj(g, 0, g, half, (proj, misc)[g % 2], max(g - 1, 0))
                if g + 2 < NB:
                    transpose_xn(0, g + 2)
            run_proj(4, 1, 0, 0)

            def run_scores(t, par, buf):
                qt = t % QT
                tile = slice(qt * P, (qt + 1) * P)
                qh, ql, kh, kl = (qk[:, par, i, :] for i in range(4))
                for n, (st, mov) in enumerate(((qh, kh), (qh, kl), (ql, kh))):
                    for h in range(2):
                        last = nc.tensor.matmul(score[buf][:, h, :], st[:, tile],
                                                mov[:, h * BANK:(h + 1) * BANK], start=n == 0, stop=n == 2)
                last.then_inc(score_mm, 1)

            def run_y(n, i, m, b, bank=None, after=None):
                c, part = m // 3, m % 3
                if m == 0:
                    signal, count = after or (y_scaled, n + i - 1)
                    if not isinstance(count, int) or count > 0:
                        pe.wait_ge(signal, count)
                st, mov = ((hTh, mvoh), (hTh, mvol), (hTl, mvoh))[part]
                t = b * QT + i
                last = nc.tensor.matmul((ybank[i % 2] if bank is None else bank)[:, :], st[:, c, t * P:(t + 1) * P], mov[:, c, :],
                                        start=m == 0, stop=m == YM - 1)
                if m == YM - 1:
                    last.then_inc(y_mm, 1)

            def run_colsum(p, par, done, what):
                pe.wait_ge(acc_done, done)
                wait_misc(p, what)
                for kt in range(QT):
                    last = nc.tensor.matmul(misc[:, kt:kt + 1], psumw[:, par, kt * P:(kt + 1) * P],
                                            ones[:, 0:1], start=True, stop=True)
                last.then_inc(misc_mm, 1)

            def wait_misc(p, what):
                if what != M_T or not isinstance(p, int) or p > 0:
                    pe.wait_ge(misc_free, misc_n(p, what) - 1)

            def run_wvT(p):
                pe.wait_ge(wqkv_in, p * 48 + 48)
                wait_misc(p, M_T)
                for a in range(2):
                    for c in range(DC):
                        at = (a * DC + c) * P
                        last = nc.tensor.transpose(misc[:, at:at + P], wraw[:, 2, c, a * DH:(a + 1) * DH],
                                                   ident[:, :])
                last.then_inc(misc_mm, 1)

            def run_mvo(p, c, what):
                pe.wait_ge(wo_lo, p + 1)
                wait_misc(p, what)
                for a in range(2):
                    last = three(misc[:, a * D:(a + 1) * D], wvTh[:, a, c, :], wvTl[:, a, c, :],
                                 woh[:, a, :], wol[:, a, :], True, True)
                last.then_inc(misc_mm, 1)

            def run_ffn_transposes(k):
                if k == 0:
                    pe.wait_ge(gate_read, 2)
                    pe.wait_ge(ffnw_f, GU + DC)
                if k >= 2:
                    pe.wait_ge(ffnw_lo, k - 1)
                bank, dst = ffn_banks[k], ybank[k % 2]
                if bank[0] == "gu":
                    _, c, s, n = bank
                    for i in range(n):
                        last = nc.tensor.transpose(dst[:, i * P:(i + 1) * P],
                                                   wgu_f[:, s + i, c * P:(c + 1) * P], ident[:, :])
                else:
                    _, k0, n, rows = bank
                    for i in range(n):
                        for c in range(DC):
                            last = nc.tensor.transpose(
                                dst[0:rows, i * D + c * P:i * D + (c + 1) * P],
                                wdraw[:, c, (k0 + i) * P:(k0 + i) * P + rows], ident[:, :])
                last.then_inc(ffnw_mm, 1)

            def pair(p, first, last):
                for t in range(STEPS):
                    j, qt = t // QT, t % QT
                    ahead, g, half = proj_at(t)
                    if qt == CSTEP and not (first and j == 0):
                        what = (-1, M_C0, M_C1, M_C2)[j]
                        run_colsum(p, (j - 1) % 2, p * STEPS + j * QT, what)
                    if qt == 0:
                        if first and j == 0:
                            pe.wait_ge(first_lo, 4)
                        else:
                            pe.wait_ge(proj_lo, p * (4 * UNITS) + 4 * j)
                    if not (first and t < 2):
                        pe.wait_ge(exp_done, p * STEPS + t - 1)
                    run_scores(t, j % 2, t % 2)
                    if not (last and ahead >= UNITS):
                        if ahead >= UNITS and g == half == 0:
                            pe.wait_ge(wqk_lo, p * 2 + 3 + (ahead - UNITS))
                        run_proj(p * (4 * UNITS) + 4 * ahead + g, ahead % UNITS, g, half)
                    phase, ms = y_matmuls(t)
                    if not (first and phase == 0):
                        for m in ms:
                            if phase and m == 0:
                                pe.wait_ge(misc_free, misc_n(p, M_M0))
                                if first:
                                    pe.wait_ge(ffnw_lo, len(ffn_banks))
                            if phase and m == 3:
                                pe.wait_ge(misc_free, misc_n(p, M_M1))
                            run_y(y_count(p, phase), m // YM, m % YM, 1 - phase)
                    k = t - FFN_AT
                    if first and 0 <= k < len(ffn_banks):
                        run_ffn_transposes(k)
                    if t == T_AT:
                        run_wvT(p)
                    if t == M0_AT:
                        pe.wait_ge(misc_free, misc_n(p, M_T))
                        run_mvo(p, 0, M_M0)
                    if t == M1_AT:
                        run_mvo(p, 1, M_M1)

            pair(0, True, False)
            with pe.Fori(1, PAIRS - 1) as p:
                pair(p, False, False)
            pair(PAIRS - 1, False, True)
            n = y_count(PAIRS, 0)
            exps = [(exp_done, PAIRS * STEPS - 1), (exp_done, PAIRS * STEPS)]
            after = [None, None, (proj_read, PAIRS * 4 * UNITS), exps[0], exps[0], exps[1], exps[1],
                     (y_scaled, n + 1)]
            for i in range(QT):
                if i == 5:
                    run_colsum(PAIRS - 1, (UNITS - 1) % 2, PAIRS * STEPS, M_C3)
                for m in range(YM):
                    run_y(n, i, m, 1, ylast[i], after[i])

            def gate_up(nb):
                cols = slice(nb * BANK, (nb + 1) * BANK)
                for k in range(HK):
                    n = nb * HK + k
                    if n >= 2:
                        pe.wait_ge(act_done, n - 1)
                    for half, slot in enumerate((k, HF + k) if k < HF else (2 * HF,)):
                        for c in range(DC):
                            last = three(four[2 * (n % 2) + half], wguh[:, c, slot * P:(slot + 1) * P],
                                         wgul[:, c, slot * P:(slot + 1) * P], hTh[:, c, cols],
                                         hTl[:, c, cols], c == 0, c == DC - 1)
                    last.then_inc(gu_mm, 1)

            def run_down(nb):
                if nb:
                    pe.wait_ge(down_free, TB * nb)
                for ks in (range(HF), range(HF, HK)):
                    for t in range(TB):
                        tile = slice(t * P, (t + 1) * P)
                        for k in ks:
                            rows = P if k < HF else HR
                            if t == 0:
                                pe.wait_ge(act_lo, nb * HK + k + 1)
                            last = three(down[t], acth[0:rows, k, tile], actl[0:rows, k, tile],
                                         wdh[0:rows, k, :], wdl[0:rows, k, :], k == 0, k == HK - 1)
                        if k == HK - 1:
                            last.then_inc(down_mm, 1)

            pe.wait_ge(y_scaled, n + 5)
            transpose_xn(1, 0)
            pe.wait_ge(y_scaled, n + QT)
            for nb in range(NB):
                pe.wait_ge(hT_lo, NB * DC + (nb + 1) * DC)
                gate_up(nb)
                if nb + 1 < NB:
                    transpose_xn(1, nb + 1)
                run_down(nb)

        @block.vector
        def _(dve):
            links = [0]

            def link(ins):
                links[0] += 1
                ins.then_inc(dve_chain, 1)
                dve.wait_ge(dve_chain, links[0])

            dve.wait_ge(siluc_done, 1)
            nc.vector.tensor_copy(scbc, siluc[:, :, :].unsqueeze(3).broadcast_to([P, DC, B, P]))\
              .then_inc(scbc_done, 1)

            def statistics(n):
                tiles = range(n * TB, (n + 1) * TB)
                for t in tiles:
                    last = nc.vector.bn_stats(stats[:, t, :], x[:, t, :])
                link(last)
                for t in tiles:
                    last = nc.vector.bn_aggr(mv[:, t, :], stats[:, t, :])
                link(last)
                at = slice(tiles[0], tiles[-1] + 1)
                nc.vector.tensor_scalar_add(mv[:, at, 1], mv[:, at, 1], EPS).then_inc(stats_done, 1)

            def normalise(m, n):
                dve.wait_ge(rstd_done, m * NB + n + 1)
                if m * NB + n not in (0, 1, NB):
                    dve.wait_ge(xnT_mm, (m * NB + n) * DC)
                for t in range(TB):
                    tt = n * TB + t
                    nc.vector.tensor_scalar(xn_of(m, n)[:, t, :], x[:, tt, :], mv[:, tt, 0:1],
                                            rstd[:, tt:tt + 1], ALU.subtract, ALU.mult).then_inc(xn_done, 1)

            def mod_out(m):
                dve.wait_ge(mod_mm, m + 1)
                mod_ps = misc[:, 0:2 * DC * B].rearrange("p (n c b) -> p n c b", n=2, c=DC)
                link(nc.vector.tensor_copy(modc[:, 2 * m, :, :], mod_ps[:, 0, :, :]))
                nc.vector.tensor_scalar_add(modc[:, 2 * m + 1, :, :], mod_ps[:, 1, :, :], 1.0)\
                  .then_inc(mod_done, 1)

            def split_hT(m, n):
                cols = slice(n * BANK, (n + 1) * BANK)
                for c in range(DC):
                    i = m * NB * DC + n * DC + c
                    dve.wait_ge(hT_hi, i + 1)
                    nc.vector.tensor_tensor(hTl[:, c, cols], htmp[:, i % 2, :], f32(hTh[:, c, cols]),
                                            ALU.subtract).then_inc(hT_lo, 1)

            def first_split(g):
                w, cols = g // 2, slice(g % 2 * BANK, (g % 2 + 1) * BANK)
                dve.wait_ge(proj_hi, g + 1)
                nc.vector.tensor_tensor(qk[:, 0, 2 * w + 1, cols], praw[:, g % 2, :],
                                        f32(qk[:, 0, 2 * w, cols]), ALU.subtract).then_inc(first_lo, 1)

            def gate_guard():
                dve.wait_ge(gate_read, 2)
                g = gtmp.rearrange("p g b d -> p (g b d)")
                out = gates[:, :, :, :].rearrange("p g b d -> p (g b d)")
                link(nc.vector.scalar_tensor_tensor(out, g, -1.0, g, ALU.mult, ALU.max))
                yield
                link(nc.vector.tensor_scalar_max(out, out, GATE_MIN))
                yield
                link(nc.vector.tensor_scalar(g, g, 0.0, 2.0, ALU.is_ge, ALU.mult))
                yield
                link(nc.vector.scalar_tensor_tensor(out, g, -1.0, out, ALU.add, ALU.mult))
                yield

            for n in range(2):
                dve.wait_ge(x_in[n], 16)
                statistics(n)
            normalise(0, 0)
            mod_out(0)
            normalise(0, 1)
            dve.wait_ge(x_in[2], 16)
            statistics(2)
            split_hT(0, 0)
            mod_out(1)
            split_hT(0, 1)
            dve.wait_ge(x_in[3], 16)
            statistics(3)
            normalise(0, 2)
            first_split(0)
            split_hT(0, 2)
            normalise(0, 3)
            first_split(1)
            split_hT(0, 3)
            first_split(2)
            first_split(3)
            guard = gate_guard()

            def run_max(p, t):
                dve.wait_ge(score_mm, p * STEPS + t + 1)
                nc.vector.tensor_reduce(nmax[:, t % 4:t % 4 + 1], score[t % 2][:, :, :], AX.XY, ALU.max,
                                        negate=True).then_inc(max_done, 1)

            def run_acc(p, t):
                s, par, buf = t % STEPS, (t % STEPS) // QT % 2, t % 4
                dve.wait_ge(rz_done, p * STEPS + t + 1)
                if s % QT == 0:
                    last = nc.vector.tensor_scalar_mul(psumw[:, par, :], prob[:, buf, :], rz[:, buf:buf + 1])
                else:
                    dve.wait_ge(acc_done, p * STEPS + t)
                    last = nc.vector.scalar_tensor_tensor(psumw[:, par, :], prob[:, buf, :],
                                                          rz[:, buf:buf + 1], psumw[:, par, :],
                                                          ALU.mult, ALU.add)
                last.then_inc(acc_done, 1)

            def run_rz(p, t):
                dve.wait_ge(exp_done, p * STEPS + t + 1)
                nc.vector.reciprocal(rz[:, t % 4:t % 4 + 1], zsum[:, t % 4:t % 4 + 1]).then_inc(rz_done, 1)

            def colsum_out(p, what, unit):
                dve.wait_ge(misc_mm, misc_n(p, what))
                nc.vector.tensor_copy(colsum[:, unit, :], misc[:, 0:QT]).then_inc(misc_free, 1)

            def misc_lo(n, lo, hi):
                dve.wait_ge(misc_hi, n + 1)
                nc.vector.tensor_tensor(lo, misc[:, :], f32(hi), ALU.subtract).then_inc(misc_free, 1)

            def pair(p, first, last):
                for t in range(STEPS):
                    j, qt = t // QT, t % QT
                    if qt == CSTEP and not (first and j == 0):
                        colsum_out(p, (-1, M_C0, M_C1, M_C2)[j], (j - 1) % UNITS)
                    run_max(p, t)
                    if t == T_EV:
                        misc_lo(p * 3, flat(wvTl), flat(wvTh))
                    if t == M0_EV:
                        misc_lo(p * 3 + 1, mvol[:, 0, :], mvoh[:, 0, :])
                    if t == M1_EV:
                        misc_lo(p * 3 + 2, mvol[:, 1, :], mvoh[:, 1, :])
                    k = t - 1 - FFN_AT
                    if first and 0 <= k < len(ffn_banks):
                        rows, cols, hi, lo = ffn_views(ffn_banks[k])
                        dve.wait_ge(ffnw_hi, k + 1)
                        nc.vector.tensor_tensor(lo, ybank[k % 2][0:rows, 0:cols], f32(hi), ALU.subtract)\
                          .then_inc(ffnw_lo, 1)
                    if first and t >= 1:
                        next(guard, None)
                    if not (first and t < 2):
                        run_acc(p, t - 2)
                    if not (first and t < 1):
                        run_rz(p, t - 1)

            def flat(ap):
                return ap[:, :, :, :].rearrange("p a c n -> p (a c n)")

            pair(0, True, False)
            with dve.Fori(1, PAIRS - 1) as p:
                pair(p, False, False)
            pair(PAIRS - 1, False, True)
            run_acc(PAIRS, -2)
            run_rz(PAIRS, -1)
            run_acc(PAIRS, -1)
            colsum_out(PAIRS - 1, M_C3, UNITS - 1)

            def residual(n):
                b = n // (NB // B)
                for t in range(n * TB, (n + 1) * TB):
                    dve.wait_ge(y_added, (y_count(PAIRS - 1 + b, 1 - b) + t % QT + 1) * 2)
                    last = nc.vector.tensor_tensor(attn[:, t, :], attn[:, t, :], gates[:, 0, b, :], ALU.mult)
                link(last)
                for t in range(n * TB, (n + 1) * TB):
                    last = nc.vector.tensor_tensor(x[:, t, :], x[:, t, :], attn[:, t, :], ALU.add)
                link(last)
                statistics(n)

            def ffn_mult(n):
                k = n % HK
                rows = P if k < HF else HR
                up = four[2 * (n % 2) + 1] if k < HF else four[2 * (n % 2)][HR:2 * HR, :]
                dve.wait_ge(sil_done, n + 1)
                if n >= 2:
                    dve.wait_ge(act_lo, n - 1)
                nc.vector.tensor_tensor(act32[0:rows, n % 2, :], up[0:rows, :], silg[0:rows, n % 2, :],
                                        ALU.mult).then_inc(act_done, 1)

            def finish(nb):
                for i in range(TB):
                    t = nb * TB + i
                    dve.wait_ge(down_mm, t + 1)
                    nc.vector.tensor_tensor(attn[:, t, :], down[i], gates[:, 1, t // QT, :], ALU.mult)\
                      .then_inc(down_free, 1)
                    dve.wait_ge(down_free, t + 1)
                    nc.vector.tensor_tensor(attn[:, t, :], attn[:, t, :], x[:, t, :], ALU.add)\
                      .then_inc(out_done, 1)

            def mults(nb):
                for k in range(HK):
                    ffn_mult(nb * HK + k)

            residual(0)
            normalise(1, 0)
            residual(1)
            split_hT(1, 0)
            normalise(1, 1)
            mults(0)
            split_hT(1, 1)
            residual(2)
            normalise(1, 2)
            finish(0)
            mults(1)
            split_hT(1, 2)
            residual(3)
            normalise(1, 3)
            finish(1)
            mults(2)
            split_hT(1, 3)
            finish(2)
            mults(3)
            finish(3)


_INS = ["L0_attn_x", "L0_attn_w_qkv", "L0_attn_w_o", "L0_ffn_wq_gate", "L0_ffn_s_gate", "L0_ffn_wq_up",
        "L0_ffn_s_up", "L0_ffn_wq_down", "L0_ffn_s_down", "L0_c", "L0_wmod"]


def kernel(**inputs):
    import numpy as np
    import concourse.bacc as bacc
    from concourse.bass_utils import run_bass_kernel_spmd

    nc = bacc.Bacc("TRN2", target_bir_lowering=False, num_devices=1)
    arrays, args = {}, []
    for name in _INS:
        a = np.ascontiguousarray(inputs[name])
        arrays[f"in_{name}"] = a
        args.append(nc.dram_tensor(f"in_{name}", a.shape, mybir.dt.from_np(a.dtype), kind="ExternalInput").ap())
    x = inputs["L0_attn_x"]
    args.append(nc.dram_tensor("out", x.shape, F32, kind="ExternalOutput").ap())
    adaln_block(nc, *args)
    r = run_bass_kernel_spmd(nc, [arrays], core_ids=[0])
    return r.results[0]["out"]
```

```python
from contextlib import ExitStack

import concourse.bass as bass
from concourse import mybir

F32 = mybir.dt.float32
F32R = mybir.dt.float32r
I32 = mybir.dt.int32
ALU = mybir.AluOpType
ACT = mybir.ActivationFunctionType
AX = mybir.AxisListType

P = 128
BANK = 512
EPS = 1e-5
ZERO_POINT = 128.0
GATE_MIN = 0.25


def adaln_block(nc, x_d, w_qkv_d, w_o_d, wq_gate_d, s_gate_d, wq_up_d, s_up_d, wq_down_d, s_down_d,
                c_d, wmod_d, out_d):
    B, S, D = x_d.shape
    DH = 128
    NH = w_o_d.shape[0] // DH
    HID = wq_gate_d.shape[0]
    SCALE = float(DH) ** -0.5
    DC = D // P
    QT = S // P
    NT = B * QT
    PAIRS = NH // 2
    UNITS = 2 * B
    STEPS = UNITS * QT
    HF = HID // P
    HR = HID - HF * P
    HK = HF + 1
    GU = 2 * HF + 1
    TB = BANK // P
    NB = NT // TB
    assert B == 2 and D == 256 and S == 1024 and NH % 2 == 0 and HR == 64

    UNIT = [(0, 0), (1, 0), (0, 1), (1, 1)]
    CSTEP, CEV = 3, (3, 5)
    T_AT, M0_AT, M1_AT = 6, 13, 14
    T_EV, M0_EV, M1_EV = 7, 14, 15
    WO_AT, WQK_AT = 9, (2 * QT + 1, 3 * QT + 1)

    YM = 3 * DC
    YRANGE = [(0, M0_AT - 1), (M1_EV, STEPS - 1)]
    YSUM = [CSTEP, 2 * QT + CSTEP]

    def y_schedule(phase, last=False):
        t0, t1 = YRANGE[phase]
        other = {t: 2 for t in range(STEPS) if t % QT in (CSTEP, CSTEP + 1) or t == T_AT}
        if not last:
            other.update({t: 3 + other.get(t, 0) for t in range(STEPS - QT - 1, STEPS)})
        done = {t0 - 1: 0}
        for t in range(t0, t1 + 1):
            goal, end = (2 * YM, YSUM[phase] + 1) if t <= YSUM[phase] + 1 else (QT * YM, t1)
            load = goal - done[t - 1] + sum(other.get(u, 0) for u in range(t, end + 1))
            n = max(0, -(-load // (end - t + 1)) - other.get(t, 0))
            done[t] = min(done[t - 1] + n, 3 if t == M1_EV else goal) if t < end else goal
        return done

    YDONE = [y_schedule(phase) for phase in range(2)]
    YDONE_LAST = [y_schedule(phase, True) for phase in range(2)]

    def y_matmuls(t, last=False):
        for phase, (t0, t1) in enumerate(YRANGE):
            if t0 <= t <= t1:
                done = (YDONE_LAST if last else YDONE)[phase]
                return phase, range(done[t - 1], done[t])
        return 0, range(0)

    def y_scales(t, last=False):
        tiles = []
        for phase in range(2):
            for i in range(QT):
                schedule = (YDONE_LAST if last else YDONE)[phase]
                done = min(u for u, n in schedule.items() if n >= (i + 1) * YM)
                if t == max(done + 1, YSUM[phase] + (1 if i == 1 else 0)):
                    tiles.append((phase, i))
        return tiles

    assert y_scales(STEPS) == y_scales(STEPS, True) == [(1, QT - 1)]

    ctx = ExitStack()
    with ctx:
        def sb(name, shape, dt=F32):
            return ctx.enter_context(nc.sbuf_tensor(name, shape, dt))

        def pb(name, shape):
            return ctx.enter_context(nc.psum_tensor(name, shape, F32))

        def sem(name):
            return ctx.enter_context(nc.semaphore(name))

        x = sb("x", [P, NT, D])
        hTh = sb("hTh", [P, DC, B * S], F32R)
        hTl = sb("hTl", [P, DC, B * S], F32R)
        attn = sb("attn", [P, NT, D])
        qk = sb("qk", [P, 2, 4, S], F32R)
        prob = sb("prob", [P, 4, S])
        psumw = sb("psumw", [P, 2, S])
        praw = sb("praw", [P, 2, BANK])
        ysc = sb("ysc", [P, 2, 2 * D])
        wraw = sb("wraw", [P, 3, DC, 2 * DH])
        woraw = sb("woraw", [P, 2, D])
        wqkh = [sb(f"wqkh{a}", [P, 2, DC, DH], F32R) for a in range(2)]
        wqkl = [sb(f"wqkl{a}", [P, 2, DC, DH], F32R) for a in range(2)]
        woh = sb("woh", [P, 2, D], F32R)
        wol = sb("wol", [P, 2, D], F32R)
        wvTh = sb("wvTh", [P, 2, DC, P], F32R)
        wvTl = sb("wvTl", [P, 2, DC, P], F32R)
        mvoh = sb("mvoh", [P, DC, 2 * D], F32R)
        mvol = sb("mvol", [P, DC, 2 * D], F32R)
        wguh = sb("wguh", [P, DC, GU * P], F32R)
        wgul = sb("wgul", [P, DC, GU * P], F32R)
        wdh = sb("wdh", [P, HK, D], F32R)
        wdl = sb("wdl", [P, HK, D], F32R)
        wdraw = sb("wdraw", [P, DC, HID])
        ident = sb("ident", [P, P])
        gates = sb("gates", [P, 2, B, D])
        modc = sb("modc", [P, 4, DC, B])
        cT = sb("cT", [P, DC, B])
        siluc = sb("siluc", [P, DC, B])
        sgu = sb("sgu", [P, GU])
        sdn = sb("sdn", [P, DC])
        stats = sb("stats", [P, NT, 6])
        mv = sb("mv", [P, NT, 2])
        minus_half = sb("minus_half", [P, TB])
        rstd = sb("rstd", [P, NT])
        nmax = sb("nmax", [P, 4])
        zsum = sb("zsum", [P, 4])
        rz = sb("rz", [P, 4])
        colsum = sb("colsum", [P, UNITS, QT])

        wmod = prob[:, 0:3, :].rearrange("p a n -> p (a n)").rearrange("p (c n) -> p c n", c=DC)
        gtmp = wraw[:, 0:2, :, :].rearrange("p w c n -> p (w c n)")
        htmp = [attn[:, NT - TB:NT, :].rearrange("p (a t) d -> p a (t d)", a=2),
                gtmp.rearrange("p (a n) -> p a n", a=2)]
        xn_praw, xn_ysc = (m[:, :, :].rearrange("p a n -> p (a n)").rearrange("p (t d) -> p t d", t=TB)
                           for m in (praw, ysc))
        xn_prob = prob[:, 3, :].rearrange("p (t d) -> p t d", t=TB)
        scbc = woraw[:, :, :].rearrange("p a n -> p (a n)").rearrange("p (c b n) -> p c b n", c=DC, b=B)
        wgate = gates[:, :, :, :]
        wgu_f = attn[:, 0:GU, :]
        wgu_i = attn[:, 0:GU, :].bitcast(I32)
        wd_i = wdraw[:, :, :].bitcast(I32)
        acth = qk[:, 0, 0:3, :].rearrange("p a n -> p (a n)").rearrange("p (k n) -> p k n", k=HK)
        actl = qk[:, 1, 0:3, :].rearrange("p a n -> p (a n)").rearrange("p (k n) -> p k n", k=HK)
        ffnraw = ysc[:, :, :]
        silg = prob[:, 0, :].rearrange("p (a n) -> p a n", a=2)
        act32 = prob[:, 1, :].rearrange("p (a n) -> p a n", a=2)

        score = [pb(f"score{i}", [P, 2, BANK]) for i in range(2)]
        proj = pb("proj", [P, BANK])
        misc = pb("misc", [P, BANK])
        ybank = [pb(f"ybank{i}", [P, BANK]) for i in range(2)]
        four = [score[0][:, 0, :], score[0][:, 1, :], score[1][:, 0, :], score[1][:, 1, :]]
        YP = QT // 2
        ylast = [ybank[0], proj, four[0], four[1], ybank[1], ybank[0], proj, ybank[1]]
        down = [ybank[0][:, 0:D], ybank[1][:, 0:D], proj[:, 0:D], misc[:, 0:D]]

        x_in = [sem(f"x_in{i}") for i in range(NB)]
        c_in, ffnw_in = sem("c_in"), sem("ffnw_in")
        wmod_in = [sem(f"wmod_in{m}") for m in range(2)] + [sem("wmodg_in")]
        wqkv_in, wo_in = sem("wqkv_in"), sem("wo_in")
        stored = sem("stored")
        const_done, pool_chain, dve_chain = sem("const_done"), sem("pool_chain"), sem("dve_chain")
        siluc_done, scbc_done, mod_mm, gate_mm, gate_read, mod_done = (sem(n) for n in (
            "siluc_done", "scbc_done", "mod_mm", "gate_mm", "gate_read", "mod_done"))
        gates_done = sem("gates_done")
        stats_done, rstd_done, xn_done = sem("stats_done"), sem("rstd_done"), sem("xn_done")
        xnT_mm, hT_hi, hT_lo = sem("xnT_mm"), sem("hT_hi"), sem("hT_lo")
        wqk_hi, wqk_lo, wo_hi, wo_lo = sem("wqk_hi"), sem("wqk_lo"), sem("wo_hi"), sem("wo_lo")
        proj_mm, proj_read, proj_hi, first_lo, proj_lo = (sem(n) for n in (
            "proj_mm", "proj_read", "proj_hi", "first_lo", "proj_lo"))
        score_mm, max_done, exp_done, rz_done, acc_done = (sem(n) for n in (
            "score_mm", "max_done", "exp_done", "rz_done", "acc_done"))
        sums_mm, sums_done = sem("sums_mm"), sem("sums_done")
        wvo_mm, wvo_hi, wvo_lo = sem("wvo_mm"), sem("wvo_hi"), sem("wvo_lo")
        y_mm, y_scaled, y_added, y_direct, resid_done = (sem(n) for n in (
            "y_mm", "y_scaled", "y_added", "y_direct", "resid_done"))
        ffnw_f, ffnw_mm, ffnw_read, ffnw_hi, ffnw_lo, ffnw_split, attn_zero = (sem(n) for n in (
            "ffnw_f", "ffnw_mm", "ffnw_read", "ffnw_hi", "ffnw_lo", "ffnw_split", "attn_zero"))
        gu_mm, sil_done, act_done, act_hi, act_lo = (sem(n) for n in (
            "gu_mm", "sil_done", "act_done", "act_hi", "act_lo"))
        down_mm, down_free, out_done = sem("down_mm"), sem("down_free"), sem("out_done")

        def f32(ap):
            return ap.bitcast(F32)

        WVO = 1 + DC

        def y_count(p, phase):
            return p * 2 * QT + (0 if phase else -QT)

        def sums_count(p, j, half):
            return p * (2 * UNITS) + 2 * j + half + 1

        def xn_of(m, n):
            return (xn_praw, xn_ysc, xn_ysc, xn_prob)[n] if m == 0 else xn_praw

        def xnT_bank(m, n, c):
            if m == 0 and n >= 2:
                return (misc, ybank[0], ybank[1], misc)[(n - 2) * DC + c][:, :]
            return four[n * DC + c] if m == 0 else four[DC + c]

        def proj_at(t):
            return (t + 1) // QT + 1, (t + 1) % QT // 2, (t + 1) % 2

        ffn_banks = [("gu", c, s, min(4, GU - s)) for c in range(DC) for s in range(0, GU, 4)]
        ffn_banks += [("dn", k, min(2, HF - k), P) for k in range(0, HF, 2)] + [("dn", HF, 1, HR)]
        FFN_AT = dict(enumerate((4, 6, 7, 9, 11, 12, 14, 16, 22, 24)))
        FFN_OF = {t: k for k, t in FFN_AT.items()}
        FFN_Y = 2 * -(-GU // 4)
        GATE_AT = (3, 5)
        assert len(ffn_banks) == len(FFN_AT) and DC == 2

        HT_AT = {2: 0, 3: 1}
        GUARD_AT = (4, 6, 8, 10)
        STAT_AT, NORM_AT = 28, 30

        def gu_bank(n, half):
            return four[2 * ((n + 1) % 2) + half]

        def ffn_views(bank):
            if bank[0] == "gu":
                _, c, s, n = bank
                return P, n * P, wguh[:, c, s * P:(s + n) * P], wgul[:, c, s * P:(s + n) * P]
            _, k, n, rows = bank
            return (rows, n * D, wdh[0:rows, k:k + n, :].rearrange("p k d -> p (k d)"),
                    wdl[0:rows, k:k + n, :].rearrange("p k d -> p (k d)"))

        qkv_v = w_qkv_d.rearrange("(c p) (w n) -> w p c n", p=P, w=3)
        wo_v = w_o_d.rearrange("(h d) n -> d h n", d=DH)
        x_v = x_d.rearrange("b (t p) d -> p (b t) d", p=P)
        out_v = out_d.rearrange("b (t p) d -> p (b t) d", p=P)

        block = ctx.enter_context(nc.Block())

        @block.sync
        def _(sp):
            def load_qkv(p):
                for w in range(3):
                    sp.dma_start(wraw[:, w, :, :], qkv_v[w, :, :, bass.ds(p * (2 * DH), 2 * DH)])\
                      .then_inc(wqkv_in, 16)

            def load_wo(p):
                sp.dma_start(woraw[:, :, :], wo_v[:, bass.ds(p * 2, 2), :]).then_inc(wo_in, 16)

            def load_x(n):
                sp.dma_start(x[:, n * TB:(n + 1) * TB, :], x_v[:, n * TB:(n + 1) * TB, :])\
                  .then_inc(x_in[n], 16)

            def load_wmod(kind, n, signal):
                cols = slice(kind * D, (kind + n) * D)
                sp.dma_start(wmod[:, :, cols], wmod_v[:, :, cols]).then_inc(signal, 16)

            wmod_v = wmod_d.rearrange("(c p) n -> p c n", p=P)
            load_x(0)
            with nc.allow_non_contiguous_dma(reason="a few hundred words, once"):
                for c in range(DC):
                    sp.dma_start(cT[:, c, :], c_d[:, c * P:(c + 1) * P].rearrange("b p -> p b"))\
                      .then_inc(c_in, 16)
            load_wmod(0, 2, wmod_in[0])
            load_x(1)
            load_qkv(0)
            load_wmod(3, 2, wmod_in[1])
            load_x(2)
            load_x(3)
            for n, kind in enumerate((2, 5)):
                sp.dma_start(wgate[:, n, :, :], wmod_v[:, :, kind * D:(kind + 1) * D]).then_inc(wmod_in[2], 16)
            for n, (w_d, s_d) in enumerate(((wq_gate_d, s_gate_d), (wq_up_d, s_up_d))):
                rem = slice(n * HR, (n + 1) * HR)
                sp.dma_start(wgu_i[:, n * HF:(n + 1) * HF, :],
                             w_d[0:HF * P, :].rearrange("(k p) d -> p k d", p=P)).then_inc(ffnw_in, 16)
                sp.dma_start(wgu_i[rem, 2 * HF, :], w_d[HF * P:HID, :]).then_inc(ffnw_in, 16)
                with nc.allow_non_contiguous_dma(reason="one scale per row"):
                    sp.dma_start(sgu[:, n * HF:(n + 1) * HF],
                                 s_d[0:HF * P].rearrange("(k p) -> p k", p=P)).then_inc(ffnw_in, 16)
                    sp.dma_start(sgu[rem, 2 * HF:GU],
                                 s_d[HF * P:HID].rearrange("(p a) -> p a", a=1)).then_inc(ffnw_in, 16)
            sp.dma_start(wd_i, wq_down_d.rearrange("(c p) k -> p c k", p=P)).then_inc(ffnw_in, 16)
            with nc.allow_non_contiguous_dma(reason="one scale per row"):
                sp.dma_start(sdn[:, :], s_down_d.rearrange("(c p) -> p c", p=P)).then_inc(ffnw_in, 16)

            sp.wait_ge(gate_mm, 2)
            load_wo(0)

            def next_pair(p):
                sp.wait_ge(wvo_mm, p * WVO + 1)
                sp.wait_ge(wqk_lo, p * 2 + 2)
                load_qkv(p + 1)
                sp.wait_ge(wo_lo, p + 1)
                load_wo(p + 1)

            with sp.Fori(0, PAIRS - 1) as p:
                next_pair(p)
            for t in range(NT):
                sp.wait_ge(out_done, t + 1)
                sp.dma_start(out_v[:, t, :], attn[:, t, :]).then_inc(stored, 16)
            sp.wait_ge(stored, 16 * NT)

        @block.gpsimd
        def _(pool):
            nc.gpsimd.memset(ident[:, :], 0.0).then_inc(pool_chain, 1)
            nc.gpsimd.memset(minus_half[:, :], -0.5).then_inc(pool_chain, 1)
            pool.wait_ge(pool_chain, 2)
            nc.gpsimd.affine_select(out=ident[:, :], in_=ident[:, :], compare_op=ALU.not_equal, fill=1.0,
                                    base=0, pattern=[[-1, P]], channel_multiplier=1).then_inc(const_done, 1)

            def split_wqk(p, a):
                pool.wait_ge(wqk_hi, p * 2 + a + 1)
                nc.gpsimd.tensor_tensor(wqkl[a][:, :, :, :], wraw[:, 0:2, :, a * DH:(a + 1) * DH],
                                        f32(wqkh[a][:, :, :, :]), ALU.subtract).then_inc(wqk_lo, 1)

            def split_wo(p):
                pool.wait_ge(wo_hi, p + 1)
                nc.gpsimd.tensor_tensor(wol[:, :, :], woraw[:, :, :], f32(woh[:, :, :]),
                                        ALU.subtract).then_inc(wo_lo, 1)

            def proj_split(n, par, g):
                w, blk = g // 2, g % 2
                cols = slice(blk * BANK, (blk + 1) * BANK)
                pool.wait_ge(proj_hi, n + 1)
                nc.gpsimd.tensor_tensor(qk[:, par, 2 * w + 1, cols], praw[:, g % 2, :],
                                        f32(qk[:, par, 2 * w, cols]), ALU.subtract).then_inc(proj_lo, 1)

            def y_add(n, i, b):
                t = b * QT + i
                pool.wait_ge(y_scaled, n + 1)
                if i == 0:
                    pool.wait_ge(attn_zero, 1)
                for a in range(2):
                    if a:
                        pool.wait_ge(y_added, n * 2 + 1)
                    nc.gpsimd.tensor_tensor(attn[:, t, :], attn[:, t, :], ysc[:, i % 2, a * D:(a + 1) * D],
                                            ALU.add).then_inc(y_added, 1)

            def residual(t):
                if t == 0:
                    pool.wait_ge(gates_done, 1)
                pool.wait_ge(y_added, (y_count(PAIRS - 1, 1) + t + 1) * 2)
                nc.gpsimd.tensor_tensor(attn[:, t, :], attn[:, t, :], gates[:, 0, 0, :], ALU.mult)\
                  .then_inc(pool_chain, 1)
                pool.wait_ge(pool_chain, 2 + t + 1)
                nc.gpsimd.tensor_tensor(x[:, t, :], x[:, t, :], attn[:, t, :], ALU.add).then_inc(resid_done, 1)

            def rstd_block(m, n):
                tiles = slice(n * TB, (n + 1) * TB)
                pool.wait_ge(stats_done, m * NB + n + 1)
                nc.gpsimd.tensor_tensor(rstd[:, tiles], mv[:, tiles, 1], minus_half[:, :], ALU.pow)\
                  .then_inc(rstd_done, 1)

            rstd_block(0, 0)
            rstd_block(0, 1)
            for a in range(2):
                split_wqk(0, a)
            rstd_block(0, 2)
            rstd_block(0, 3)
            pool.wait_ge(ffnw_in, 10 * 16)
            for s in range(GU):
                nc.gpsimd.tensor_scalar(wgu_f[:, s, :], wgu_i[:, s, :], -ZERO_POINT, sgu[:, s:s + 1],
                                        ALU.add, ALU.mult).then_inc(ffnw_f, 1)
            for c in range(DC):
                nc.gpsimd.tensor_scalar(wdraw[:, c, :], wd_i[:, c, :], -ZERO_POINT, sdn[:, c:c + 1],
                                        ALU.add, ALU.mult).then_inc(ffnw_f, 1)

            def pair(p, first, last):
                for t in range(STEPS):
                    ahead, g, half = proj_at(t)
                    if half and not (last and ahead >= UNITS):
                        proj_split(p * (4 * UNITS) + 4 * ahead + g, ahead % 2, g)
                    if first and FFN_OF.get(t - 1, FFN_Y) < FFN_Y:
                        k = FFN_OF[t - 1]
                        rows, cols, hi, lo = ffn_views(ffn_banks[k])
                        pool.wait_ge(ffnw_hi, k + 1)
                        nc.gpsimd.tensor_tensor(lo, ffnraw[0:rows, k % 2, 0:cols], f32(hi), ALU.subtract)\
                          .then_inc(ffnw_lo, 1)
                    if t == WO_AT:
                        split_wo(p)
                    if t in WQK_AT and not last:
                        split_wqk(p + 1, WQK_AT.index(t))
                    if first and t == YRANGE[1][0]:
                        pool.wait_ge(ffnw_mm, FFN_Y)
                        nc.gpsimd.memset(attn[:, :, :], 0.0).then_inc(attn_zero, 1)
                    if t == 0 and not first:
                        y_add(y_count(p, 0) - 1, QT - 1, 0)
                    for phase, tile in y_scales(t, last):
                        if not (first and phase == 0):
                            y_add(y_count(p, phase) + tile, tile, 1 - phase)
                            if last and phase:
                                residual(tile)
                    if last and t == STAT_AT:
                        rstd_block(1, 0)

            pair(0, True, False)
            with pool.Fori(1, PAIRS - 1) as p:
                pair(p, False, False)
            pair(PAIRS - 1, False, True)
            y_add(y_count(PAIRS, 0) - 1, QT - 1, 0)
            residual(QT - 1)
            for i in range(YP):
                y_add(y_count(PAIRS, 0) + i, i, 1)
            rstd_block(1, 1)
            for n in range(NB * HK):
                k = n % HK
                rows = P if k < HF else HR
                pool.wait_ge(act_hi, n + 1)
                nc.gpsimd.tensor_tensor(actl[0:rows, k, :], act32[0:rows, n % 2, :],
                                        f32(acth[0:rows, k, :]), ALU.subtract).then_inc(act_lo, 1)
                if k == HK - 1 and n // HK + 2 < NB:
                    rstd_block(1, n // HK + 2)

        @block.scalar
        def _(act):
            act.wait_ge(c_in, 16 * DC)
            nc.scalar.activation(siluc[:, :, :], cT[:, :, :], ACT.Silu).then_inc(siluc_done, 1)

            def split_wqk(p, a):
                act.wait_ge(wqkv_in, p * 48 + 48)
                nc.scalar.activation(wqkh[a][:, :, :, :], wraw[:, 0:2, :, a * DH:(a + 1) * DH], ACT.Copy)\
                  .then_inc(wqk_hi, 1)

            def hT_block(m, n, c):
                i = m * NB * DC + n * DC + c
                b = n // (NB // B)
                cols = slice(n * BANK, (n + 1) * BANK)
                act.wait_ge(mod_done, m + 1)
                act.wait_ge(xnT_mm, i + 1)
                if i >= 2:
                    act.wait_ge(hT_lo, i - 1)
                for dst in (htmp[m][:, i % 2, :], hTh[:, c, cols]):
                    last = nc.scalar.activation(dst, xnT_bank(m, n, c), ACT.Identity,
                                                bias=modc[:, 2 * m, c, b:b + 1],
                                                scale=modc[:, 2 * m + 1, c, b:b + 1])
                last.then_inc(hT_hi, 1)

            def proj_out(n, par, g, bank=proj):
                w, blk = g // 2, g % 2
                act.wait_ge(proj_mm, n + 1)
                if not isinstance(n, int) or n >= 6:
                    act.wait_ge(proj_lo, n - 5)
                elif n >= 2:
                    act.wait_ge(first_lo, n - 1)
                nc.scalar.activation(praw[:, g % 2, :], bank[:, :], ACT.Copy, scale=1.0 if w else SCALE)\
                  .then_inc(proj_read, 1)
                act.wait_ge(proj_read, n + 1)
                nc.scalar.activation(qk[:, par, 2 * w, blk * BANK:(blk + 1) * BANK], praw[:, g % 2, :],
                                     ACT.Copy).then_inc(proj_hi, 1)

            def hT_blocks(m, n):
                for c in range(DC):
                    hT_block(m, n, c)

            for a in range(2):
                split_wqk(0, a)
            for n in range(2):
                hT_blocks(0, n)
            for g in range(4):
                proj_out(g, 0, g, (proj, misc)[g % 2])
            hT_blocks(0, 2)

            def y_scale(n, i, b, sums, bank=None):
                act.wait_ge(y_mm, n + 1)
                if i % (QT // 2) == 0:
                    act.wait_ge(sums_done, sums + (i > 0))
                if not isinstance(n, int) or n >= 2:
                    act.wait_ge(y_added, n * 2 - 2)
                bank = ybank[i % 2] if bank is None else bank
                for a in range(2):
                    last = nc.scalar.activation(ysc[:, i % 2, a * D:(a + 1) * D],
                                                bank[:, a * D:(a + 1) * D], ACT.Copy,
                                                scale=colsum[:, 2 * b + a, i:i + 1])
                last.then_inc(y_scaled, 1)

            def sum_rows(n, unit, half):
                act.wait_ge(sums_mm, n)
                for i in range(QT // 2):
                    at = half * (QT // 2) + i
                    tile = misc[:, i * P:(i + 1) * P]
                    last = nc.scalar.activation(tile, tile, ACT.Copy, accum_out=colsum[:, unit, at:at + 1])
                last.then_inc(sums_done, 1)

            def pair(p, first, last):
                for t in range(STEPS):
                    for half in range(2):
                        if t % QT == CEV[half] and not (first and t < QT):
                            j = t // QT - 1
                            sum_rows(sums_count(p, j, half), j % UNITS, half)
                    for n in range(2):
                        if first and t == GATE_AT[n] + 1:
                            act.wait_ge(gate_mm, n + 1)
                            nc.scalar.activation(gates[:, n, :, :], ybank[n][:, :], ACT.Copy)\
                              .then_inc(gate_read, 1)
                    if first and t in HT_AT:
                        hT_block(0, NB - 1, HT_AT[t])
                    if first and FFN_OF.get(t - 1, 0) >= FFN_Y:
                        k = FFN_OF[t - 1]
                        rows, cols, hi, _ = ffn_views(ffn_banks[k])
                        act.wait_ge(ffnw_mm, k + 1)
                        nc.scalar.activation(hi, misc[0:rows, 0:cols], ACT.Copy).then_inc(ffnw_hi, 1)
                    elif first and t - 1 in FFN_OF:
                        k = FFN_OF[t - 1]
                        rows, cols, hi, _ = ffn_views(ffn_banks[k])
                        raw = ffnraw[0:rows, k % 2, 0:cols]
                        act.wait_ge(ffnw_mm, k + 1)
                        if k >= 2:
                            act.wait_ge(ffnw_lo, k - 1)
                        nc.scalar.activation(raw, ybank[k % 2][0:rows, 0:cols], ACT.Copy)\
                          .then_inc(ffnw_read, 1)
                        act.wait_ge(ffnw_read, k + 1)
                        nc.scalar.activation(hi, raw, ACT.Copy).then_inc(ffnw_hi, 1)
                    if t == 0 and not first:
                        y_scale(y_count(p, 0) - 1, QT - 1, 0, None)
                    for phase, tile in y_scales(t, last):
                        if not (first and phase == 0):
                            y_scale(y_count(p, phase) + tile, tile, 1 - phase,
                                    sums_count(p, 1 if phase else -1, 0))
                    for c, at in enumerate((M0_EV, M1_EV)):
                        if t == at:
                            act.wait_ge(wvo_mm, p * WVO + 2 + c)
                            nc.scalar.activation(mvoh[:, c, :], ybank[c][:, :], ACT.Copy).then_inc(wvo_hi, 1)
                    ahead, g, half = proj_at(t)
                    if half and not (last and ahead >= UNITS):
                        proj_out(p * (4 * UNITS) + 4 * ahead + g, ahead % 2, g)
                    if t == T_EV:
                        act.wait_ge(wvo_mm, p * WVO + 1)
                        nc.scalar.activation(wvTh[:, :, :, :], misc[:, :], ACT.Copy).then_inc(wvo_hi, 1)
                    if t == WO_AT:
                        act.wait_ge(wo_in, p * 16 + 16)
                        nc.scalar.activation(woh[:, :, :], woraw[:, :, :], ACT.Copy).then_inc(wo_hi, 1)
                    if t in WQK_AT and not last:
                        split_wqk(p + 1, WQK_AT.index(t))
                    act.wait_ge(max_done, p * STEPS + t + 1)
                    if not (first and t < 4):
                        act.wait_ge(acc_done, p * STEPS + t - 3)
                    nc.scalar.activation(prob[:, t % 4, :], score[t % 2][:, :, :], ACT.Exp,
                                         bias=nmax[:, t % 4:t % 4 + 1], scale=1.0,
                                         accum_out=zsum[:, t % 4:t % 4 + 1]).then_inc(exp_done, 1)

            pair(0, True, False)
            with act.Fori(1, PAIRS - 1) as p:
                pair(p, False, False)
            pair(PAIRS - 1, False, True)
            y_scale(y_count(PAIRS, 0) - 1, QT - 1, 0, None)
            hT_blocks(1, 0)
            for i in range(YP):
                if i < 2:
                    sum_rows(sums_count(PAIRS, -1, i), UNITS - 1, i)
                y_scale(y_count(PAIRS, 0) + i, i, 1, sums_count(PAIRS, -1, 0), ylast[i])

            def ffn_act(n):
                k = n % HK
                rows = P if k < HF else HR
                act.wait_ge(gu_mm, n + 1)
                if n >= 2:
                    act.wait_ge(act_done, n - 1)
                nc.scalar.activation(silg[0:rows, n % 2, :], gu_bank(n, 0)[0:rows, :], ACT.Silu)\
                  .then_inc(sil_done, 1)

            def ffn_hi(n):
                k = n % HK
                rows = P if k < HF else HR
                act.wait_ge(act_done, n + 1)
                nc.scalar.activation(acth[0:rows, k, :], act32[0:rows, n % 2, :], ACT.Copy)\
                  .then_inc(act_hi, 1)

            for nb in range(NB):
                if nb:
                    hT_blocks(1, nb)
                for k in range(HK):
                    ffn_act(nb * HK + k)
                    if k:
                        ffn_hi(nb * HK + k - 1)
                ffn_hi(nb * HK + HK - 1)

        @block.tensor
        def _(pe):
            def three(out, stat_hi, stat_lo, mov_hi, mov_lo, start, stop):
                nc.tensor.matmul(out, stat_hi, mov_hi, start=start, stop=False)
                nc.tensor.matmul(out, stat_hi, mov_lo, start=False, stop=False)
                return nc.tensor.matmul(out, stat_lo, mov_hi, start=False, stop=stop)

            def modulation(m):
                pe.wait_ge(wmod_in[m], 16)
                if m:
                    pe.wait_ge(mod_done, 1)
                for n, kind in enumerate((3 * m, 3 * m + 1)):
                    for c2 in range(DC):
                        at = (n * DC + c2) * B
                        for c in range(DC):
                            last = nc.tensor.matmul(misc[:, at:at + B],
                                                    wmod[:, c, kind * D + c2 * P:kind * D + (c2 + 1) * P],
                                                    siluc[:, c, :], start=c == 0, stop=c == DC - 1)
                last.then_inc(mod_mm, 1)

            def gate_rows(n):
                if n == 0:
                    pe.wait_ge(scbc_done, 1)
                    pe.wait_ge(wmod_in[2], 32)
                    pe.wait_ge(hT_hi, 3 * DC + 1)
                for b in range(B):
                    for c in range(DC):
                        last = nc.tensor.matmul(ybank[n][:, b * D:(b + 1) * D], scbc[:, c, b, :],
                                                wgate[:, n, c, :], start=c == 0, stop=c == DC - 1)
                last.then_inc(gate_mm, 1)

            def transpose_xn(m, n, chunks=range(DC)):
                pe.wait_ge(xn_done, m * NT + (n + 1) * TB)
                if m == 1 and n >= 1:
                    pe.wait_ge(act_done, n * HK - 1)
                for c in chunks:
                    for t in range(TB):
                        last = nc.tensor.transpose(xnT_bank(m, n, c)[:, t * P:(t + 1) * P],
                                                   xn_of(m, n)[:, t, c * P:(c + 1) * P], ident[:, :])
                    last.then_inc(xnT_mm, 1)

            def proj_mms(a, b, g):
                w, blk = g // 2, g % 2
                cols = slice(b * S + blk * BANK, b * S + (blk + 1) * BANK)
                return [(st[:, w, c, :], mov[:, c, cols]) for c in range(DC)
                        for st, mov in ((wqkh[a], hTh), (wqkh[a], hTl), (wqkl[a], hTh))]

            def run_proj(n, unit, g, half, bank=proj, read=None):
                a, b = UNIT[unit]
                mms = proj_mms(a, b, g)
                if half == 0 and read != 0:
                    pe.wait_ge(proj_read, n if read is None else read)
                for m in range(half * 3, half * 3 + 3):
                    last = nc.tensor.matmul(bank[:, :], *mms[m], start=m == 0, stop=m == YM - 1)
                if half:
                    last.then_inc(proj_mm, 1)

            pe.wait_ge(siluc_done, 1)
            modulation(0)
            pe.wait_ge(const_done, 1)
            transpose_xn(0, 0)
            transpose_xn(0, 1)
            modulation(1)
            pe.wait_ge(wqk_lo, 2)
            for g in range(4):
                if g < 2:
                    pe.wait_ge(hT_lo, (g + 1) * DC)
                if g == 1:
                    pe.wait_ge(mod_done, 2)
                for half in range(2):
                    run_proj(g, 0, g, half, (proj, misc)[g % 2], max(g - 1, 0))
            run_proj(4, 1, 0, 0, read=3)
            pe.wait_ge(proj_read, 4)
            transpose_xn(0, 2)

            def run_scores(t, par, buf):
                qt = t % QT
                tile = slice(qt * P, (qt + 1) * P)
                qh, ql, kh, kl = (qk[:, par, i, :] for i in range(4))
                for n, (st, mov) in enumerate(((qh, kh), (qh, kl), (ql, kh))):
                    for h in range(2):
                        last = nc.tensor.matmul(score[buf][:, h, :], st[:, tile],
                                                mov[:, h * BANK:(h + 1) * BANK], start=n == 0, stop=n == 2)
                last.then_inc(score_mm, 1)

            def run_y(n, i, m, b, bank=None, after=None):
                c, part = m // 3, m % 3
                if m == 0:
                    signal, count = after or (y_scaled, n + i - 1)
                    if not isinstance(count, int) or count > 0:
                        pe.wait_ge(signal, count)
                st, mov = ((hTh, mvoh), (hTh, mvol), (hTl, mvoh))[part]
                t = b * QT + i
                bank = ybank[i % 2] if bank is None else bank
                last = nc.tensor.matmul(bank[:, :], st[:, c, t * P:(t + 1) * P], mov[:, c, :],
                                        start=m == 0, stop=m == YM - 1)
                if m == YM - 1:
                    last.then_inc(y_mm, 1)

            def run_sums(p, j, half, ffn=0):
                if ffn:
                    pe.wait_ge(ffnw_split, ffn)
                n = sums_count(p, j, half)
                if half == 0:
                    pe.wait_ge(acc_done, p * STEPS + (j + 1) * QT)
                if half == 0 and j == 0:
                    pe.wait_ge(wvo_lo, p * WVO + 1)
                else:
                    pe.wait_ge(sums_done, n - 1)
                for i in range(QT // 2):
                    at = half * (QT // 2) + i
                    last = nc.tensor.transpose(misc[:, i * P:(i + 1) * P],
                                               psumw[:, j % 2, at * P:(at + 1) * P], ident[:, :])
                last.then_inc(sums_mm, 1)

            def run_wvT(p, first):
                pe.wait_ge(wqkv_in, p * 48 + 48)
                if not first:
                    pe.wait_ge(sums_done, sums_count(p, -1, 1))
                for a in range(2):
                    for c in range(DC):
                        at = (a * DC + c) * P
                        last = nc.tensor.transpose(misc[:, at:at + P], wraw[:, 2, c, a * DH:(a + 1) * DH],
                                                   ident[:, :])
                last.then_inc(wvo_mm, 1)

            def run_mvo(p, c, first):
                if c == 0:
                    pe.wait_ge(wo_lo, p + 1)
                    pe.wait_ge(wvo_lo, p * WVO + 1)
                if first:
                    pe.wait_ge(ffnw_read, FFN_Y - 1 + c)
                else:
                    pe.wait_ge(y_scaled, y_count(p, 1) - 1 + c)
                for a in range(2):
                    last = three(ybank[c][:, a * D:(a + 1) * D], wvTh[:, a, c, :], wvTl[:, a, c, :],
                                 woh[:, a, :], wol[:, a, :], True, True)
                last.then_inc(wvo_mm, 1)

            def run_ffn_transposes(k):
                if k < 2:
                    pe.wait_ge(gate_read, k + 1)
                    pe.wait_ge(ffnw_f, GU + DC)
                elif 2 <= k < FFN_Y:
                    pe.wait_ge(ffnw_read, k - 1)
                elif k >= FFN_Y:
                    pe.wait_ge(sums_done, sums_count(0, (FFN_AT[k] - CSTEP - 1) // QT - 1, 1))
                    if k > FFN_Y:
                        pe.wait_ge(ffnw_split, k - FFN_Y)
                bank, dst = ffn_banks[k], ybank[k % 2] if k < FFN_Y else misc
                if bank[0] == "gu":
                    _, c, s, n = bank
                    for i in range(n):
                        last = nc.tensor.transpose(dst[:, i * P:(i + 1) * P],
                                                   wgu_f[:, s + i, c * P:(c + 1) * P], ident[:, :])
                else:
                    _, k0, n, rows = bank
                    for i in range(n):
                        for c in range(DC):
                            last = nc.tensor.transpose(
                                dst[0:rows, i * D + c * P:i * D + (c + 1) * P],
                                wdraw[:, c, (k0 + i) * P:(k0 + i) * P + rows], ident[:, :])
                last.then_inc(ffnw_mm, 1)

            def pair(p, first, last):
                for t in range(STEPS):
                    j, qt = t // QT, t % QT
                    ahead, g, half = proj_at(t)
                    if qt == CSTEP and not (first and j == 0):
                        through_misc = [k for k, at in FFN_AT.items() if k >= FFN_Y and at < t]
                        run_sums(p, j - 1, 0, len(through_misc) if first else 0)
                    if qt == 0:
                        if first and j == 0:
                            pe.wait_ge(first_lo, 4)
                        else:
                            pe.wait_ge(proj_lo, p * (4 * UNITS) + 4 * j)
                    if not (first and t < 2):
                        pe.wait_ge(exp_done, p * STEPS + t - 1)
                    run_scores(t, j % 2, t % 2)
                    if not (last and ahead >= UNITS):
                        if ahead >= UNITS and g == half == 0:
                            pe.wait_ge(wqk_lo, p * 2 + 3 + (ahead - UNITS))
                        if first and ahead == 2 and g == half == 0:
                            pe.wait_ge(hT_lo, NB * DC)
                        run_proj(p * (4 * UNITS) + 4 * ahead + g, ahead % UNITS, g, half)
                    phase, ms = y_matmuls(t, last)
                    if not (first and phase == 0):
                        for m in ms:
                            if phase and m == 0:
                                pe.wait_ge(wvo_lo, p * WVO + 2)
                            if phase and m == 3:
                                pe.wait_ge(wvo_lo, p * WVO + 3)
                            run_y(y_count(p, phase), m // YM, m % YM, 1 - phase)
                    if first and t == 1:
                        transpose_xn(0, 3, (0,))
                    if first and t == 2:
                        pe.wait_ge(hT_hi, 2 * DC + 1)
                        transpose_xn(0, 3, (1,))
                    if first and t in GATE_AT:
                        gate_rows(GATE_AT.index(t))
                    if first and t in FFN_OF:
                        run_ffn_transposes(FFN_OF[t])
                    if qt == CSTEP + 1 and not (first and j == 0):
                        run_sums(p, j - 1, 1)
                    if t == T_AT:
                        run_wvT(p, first)
                    if t == M0_AT:
                        run_mvo(p, 0, first)
                    if t == M1_AT:
                        run_mvo(p, 1, first)

            pair(0, True, False)
            with pe.Fori(1, PAIRS - 1) as p:
                pair(p, False, False)
            pair(PAIRS - 1, False, True)
            def gate_up(nb, ks):
                cols = slice(nb * BANK, (nb + 1) * BANK)
                for k in ks:
                    n = nb * HK + k
                    if n >= 2:
                        pe.wait_ge(act_done, n - 1)
                    for half, slot in enumerate((k, HF + k) if k < HF else (2 * HF,)):
                        for c in range(DC):
                            last = three(gu_bank(n, half), wguh[:, c, slot * P:(slot + 1) * P],
                                         wgul[:, c, slot * P:(slot + 1) * P], hTh[:, c, cols],
                                         hTl[:, c, cols], c == 0, c == DC - 1)
                    last.then_inc(gu_mm, 1)

            def run_down(nb):
                if nb:
                    pe.wait_ge(down_free, TB * nb)
                else:
                    pe.wait_ge(y_direct, QT - YP)
                for ks in (range(HF - 2), range(HF - 2, HK)):
                    for t in range(TB):
                        tile = slice(t * P, (t + 1) * P)
                        for k in ks:
                            rows = P if k < HF else HR
                            if t == 0:
                                pe.wait_ge(act_lo, nb * HK + k + 1)
                            last = three(down[t], acth[0:rows, k, tile], actl[0:rows, k, tile],
                                         wdh[0:rows, k, :], wdl[0:rows, k, :], k == 0, k == HK - 1)
                        if k == HK - 1:
                            last.then_inc(down_mm, 1)

            n = y_count(PAIRS, 0)
            after = [(y_scaled, n - 1), (proj_read, PAIRS * 4 * UNITS), (exp_done, PAIRS * STEPS - 1),
                     (exp_done, PAIRS * STEPS - 1), (y_scaled, n), (y_scaled, n + 1),
                     (y_scaled, n + 2), (y_direct, 1)]
            for i in range(QT):
                if i == YP - 1:
                    pe.wait_ge(exp_done, PAIRS * STEPS)
                    transpose_xn(1, 0)
                if i == YP + 1:
                    run_sums(PAIRS - 1, UNITS - 1, 0)
                    pe.wait_ge(hT_lo, (NB + 1) * DC)
                    gate_up(0, (0,))
                    run_sums(PAIRS - 1, UNITS - 1, 1)
                for m in range(YM):
                    run_y(n, i, m, 1, ylast[i], after[i])
            pe.wait_ge(y_scaled, n + YP)
            for nb in range(NB):
                if nb:
                    pe.wait_ge(hT_lo, (NB + nb + 1) * DC)
                gate_up(nb, range(HK) if nb else range(1, HK))
                if nb + 1 < NB:
                    transpose_xn(1, nb + 1)
                run_down(nb)

        @block.vector
        def _(dve):
            links = [0]

            def link(ins):
                links[0] += 1
                ins.then_inc(dve_chain, 1)
                dve.wait_ge(dve_chain, links[0])

            dve.wait_ge(siluc_done, 1)
            nc.vector.tensor_copy(scbc, siluc[:, :, :].unsqueeze(3).broadcast_to([P, DC, B, P]))\
              .then_inc(scbc_done, 1)

            def statistics(n):
                tiles = range(n * TB, (n + 1) * TB)
                for t in tiles:
                    last = nc.vector.bn_stats(stats[:, t, :], x[:, t, :])
                link(last)
                for t in tiles:
                    last = nc.vector.bn_aggr(mv[:, t, :], stats[:, t, :])
                link(last)
                at = slice(tiles[0], tiles[-1] + 1)
                nc.vector.tensor_scalar_add(mv[:, at, 1], mv[:, at, 1], EPS).then_inc(stats_done, 1)

            def normalise(m, n):
                dve.wait_ge(rstd_done, m * NB + n + 1)
                if m and n or n == 2:
                    dve.wait_ge(xnT_mm, (m * NB + n) * DC)
                for t in range(TB):
                    tt = n * TB + t
                    nc.vector.tensor_scalar(xn_of(m, n)[:, t, :], x[:, tt, :], mv[:, tt, 0:1],
                                            rstd[:, tt:tt + 1], ALU.subtract, ALU.mult).then_inc(xn_done, 1)

            def mod_out(m):
                dve.wait_ge(mod_mm, m + 1)
                mod_ps = misc[:, 0:2 * DC * B].rearrange("p (n c b) -> p n c b", n=2, c=DC)
                link(nc.vector.tensor_copy(modc[:, 2 * m, :, :], mod_ps[:, 0, :, :]))
                nc.vector.tensor_scalar_add(modc[:, 2 * m + 1, :, :], mod_ps[:, 1, :, :], 1.0)\
                  .then_inc(mod_done, 1)

            def split_hT(m, n, c):
                cols = slice(n * BANK, (n + 1) * BANK)
                i = m * NB * DC + n * DC + c
                dve.wait_ge(hT_hi, i + 1)
                nc.vector.tensor_tensor(hTl[:, c, cols], htmp[m][:, i % 2, :], f32(hTh[:, c, cols]),
                                        ALU.subtract).then_inc(hT_lo, 1)

            def split_hTs(m, n):
                for c in range(DC):
                    split_hT(m, n, c)

            def first_split(g):
                w, cols = g // 2, slice(g % 2 * BANK, (g % 2 + 1) * BANK)
                dve.wait_ge(proj_hi, g + 1)
                nc.vector.tensor_tensor(qk[:, 0, 2 * w + 1, cols], praw[:, g % 2, :],
                                        f32(qk[:, 0, 2 * w, cols]), ALU.subtract).then_inc(first_lo, 1)

            def gate_guard():
                dve.wait_ge(gate_read, 2)
                g = gates[:, :, :, :].rearrange("p g b d -> p (g b d)")
                link(nc.vector.scalar_tensor_tensor(gtmp, g, -1.0, g, ALU.mult, ALU.max))
                yield
                link(nc.vector.tensor_scalar_max(gtmp, gtmp, GATE_MIN))
                yield
                link(nc.vector.tensor_scalar(g, g, 0.0, 2.0, ALU.is_ge, ALU.mult))
                yield
                nc.vector.scalar_tensor_tensor(g, g, -1.0, gtmp, ALU.add, ALU.mult).then_inc(gates_done, 1)
                yield

            for n in range(2):
                dve.wait_ge(x_in[n], 16)
                statistics(n)
            normalise(0, 0)
            mod_out(0)
            normalise(0, 1)
            split_hTs(0, 0)
            mod_out(1)
            split_hTs(0, 1)
            dve.wait_ge(x_in[2], 16)
            statistics(2)
            first_split(0)
            first_split(1)
            normalise(0, 2)
            first_split(2)
            first_split(3)
            dve.wait_ge(x_in[3], 16)
            statistics(3)
            guard = gate_guard()

            def run_max(p, t):
                dve.wait_ge(score_mm, p * STEPS + t + 1)
                nc.vector.tensor_reduce(nmax[:, t % 4:t % 4 + 1], score[t % 2][:, :, :], AX.XY, ALU.max,
                                        negate=True).then_inc(max_done, 1)

            def run_acc(p, t):
                s, par, buf = t % STEPS, (t % STEPS) // QT % 2, t % 4
                dve.wait_ge(rz_done, p * STEPS + t + 1)
                if s % QT == 0:
                    last = nc.vector.tensor_scalar_mul(psumw[:, par, :], prob[:, buf, :], rz[:, buf:buf + 1])
                else:
                    dve.wait_ge(acc_done, p * STEPS + t)
                    last = nc.vector.scalar_tensor_tensor(psumw[:, par, :], prob[:, buf, :],
                                                          rz[:, buf:buf + 1], psumw[:, par, :],
                                                          ALU.mult, ALU.add)
                last.then_inc(acc_done, 1)

            def run_rz(p, t):
                dve.wait_ge(exp_done, p * STEPS + t + 1)
                nc.vector.reciprocal(rz[:, t % 4:t % 4 + 1], zsum[:, t % 4:t % 4 + 1]).then_inc(rz_done, 1)

            def statistics2(n):
                dve.wait_ge(resid_done, (n + 1) * TB)
                statistics(n)

            def wvo_split(n, bank, lo, hi):
                dve.wait_ge(wvo_hi, n + 1)
                nc.vector.tensor_tensor(lo, bank[:, :], f32(hi), ALU.subtract).then_inc(wvo_lo, 1)

            def pair(p, first, last):
                for t in range(STEPS):
                    j, qt = t // QT, t % QT
                    run_max(p, t)
                    if first and t == 0:
                        normalise(0, 3)
                        split_hTs(0, 2)
                    if t == T_EV:
                        wvo_split(p * WVO, misc, flat(wvTl), flat(wvTh))
                    for c, at in enumerate((M0_EV, M1_EV)):
                        if t == at:
                            wvo_split(p * WVO + 1 + c, ybank[c], mvol[:, c, :], mvoh[:, c, :])
                    if first and FFN_OF.get(t - 1, 0) >= FFN_Y:
                        rows, cols, hi, lo = ffn_views(ffn_banks[FFN_OF[t - 1]])
                        dve.wait_ge(ffnw_hi, FFN_OF[t - 1] + 1)
                        nc.vector.tensor_tensor(lo, misc[0:rows, 0:cols], f32(hi), ALU.subtract)\
                          .then_inc(ffnw_split, 1)
                    if first and t in HT_AT:
                        split_hT(0, NB - 1, HT_AT[t])
                    if last and t in GUARD_AT:
                        next(guard)
                    if not (first and t < 2):
                        run_acc(p, t - 2)
                    if not (first and t < 1):
                        run_rz(p, t - 1)
                    if last and t == STAT_AT:
                        statistics2(0)
                    if last and t == NORM_AT:
                        normalise(1, 0)

            def flat(ap):
                return ap[:, :, :, :].rearrange("p a c n -> p (a c n)")

            pair(0, True, False)
            with dve.Fori(1, PAIRS - 1) as p:
                pair(p, False, False)
            pair(PAIRS - 1, False, True)
            run_acc(PAIRS, -2)
            run_rz(PAIRS, -1)
            run_acc(PAIRS, -1)

            def residual(t):
                i = t % QT
                if i < YP:
                    dve.wait_ge(y_added, (y_count(PAIRS, 0) + i + 1) * 2)
                else:
                    dve.wait_ge(y_direct, i - YP + 1)
                link(nc.vector.tensor_tensor(attn[:, t, :], attn[:, t, :], gates[:, 0, 1, :], ALU.mult))
                nc.vector.tensor_tensor(x[:, t, :], x[:, t, :], attn[:, t, :], ALU.add).then_inc(resid_done, 1)

            def add_y(i):
                t = (B - 1) * QT + i
                dve.wait_ge(y_mm, y_count(PAIRS, 0) + i + 1)
                for a in range(2):
                    last = nc.vector.scalar_tensor_tensor(
                        attn[:, t, :], ylast[i][:, a * D:(a + 1) * D], colsum[:, UNITS - 2 + a, i:i + 1],
                        attn[:, t, :], ALU.mult, ALU.add)
                    if a == 0:
                        link(last)
                last.then_inc(y_direct, 1)

            def ffn_mult(n):
                k = n % HK
                rows = P if k < HF else HR
                up = gu_bank(n, 1) if k < HF else gu_bank(n, 0)[HR:2 * HR, :]
                dve.wait_ge(sil_done, n + 1)
                if n >= 2:
                    dve.wait_ge(act_lo, n - 1)
                nc.vector.tensor_tensor(act32[0:rows, n % 2, :], up[0:rows, :], silg[0:rows, n % 2, :],
                                        ALU.mult).then_inc(act_done, 1)

            def finish(t):
                dve.wait_ge(down_mm, t + 1)
                nc.vector.tensor_tensor(attn[:, t, :], down[t % TB], gates[:, 1, t // QT, :], ALU.mult)\
                  .then_inc(down_free, 1)
                dve.wait_ge(down_free, t + 1)
                nc.vector.tensor_tensor(attn[:, t, :], attn[:, t, :], x[:, t, :], ALU.add)\
                  .then_inc(out_done, 1)

            split_hTs(1, 0)
            statistics2(1)
            dve.wait_ge(y_added, y_count(PAIRS, 0) * 2)
            dve.wait_ge(sums_done, sums_count(PAIRS, -1, 1))
            add_y(YP)
            for i in range(YP + 1, QT):
                add_y(i)
            for nb in range(NB):
                for k in range(HK):
                    ffn_mult(nb * HK + k)
                    if nb == 0 and k < TB:
                        residual(QT + k)
                    if k == 2 and nb + 1 < NB:
                        normalise(1, nb + 1)
                    if nb and k in (0, 1, 3, 4):
                        finish((nb - 1) * TB + (0, 1, 3, 4).index(k))
                if nb + 1 < NB:
                    split_hTs(1, nb + 1)
                if nb == 0:
                    statistics2(2)
                    for t in range(QT + TB, NT):
                        residual(t)
                    statistics2(3)
            for t in range((NB - 1) * TB, NT):
                finish(t)


_INS = ["L0_attn_x", "L0_attn_w_qkv", "L0_attn_w_o", "L0_ffn_wq_gate", "L0_ffn_s_gate", "L0_ffn_wq_up",
        "L0_ffn_s_up", "L0_ffn_wq_down", "L0_ffn_s_down", "L0_c", "L0_wmod"]


def kernel(**inputs):
    import numpy as np
    import concourse.bacc as bacc
    from concourse.bass_utils import run_bass_kernel_spmd

    nc = bacc.Bacc("TRN2", target_bir_lowering=False, num_devices=1)
    arrays, args = {}, []
    for name in _INS:
        a = np.ascontiguousarray(inputs[name])
        arrays[f"in_{name}"] = a
        args.append(nc.dram_tensor(f"in_{name}", a.shape, mybir.dt.from_np(a.dtype), kind="ExternalInput").ap())
    x = inputs["L0_attn_x"]
    args.append(nc.dram_tensor("out", x.shape, F32, kind="ExternalOutput").ap())
    adaln_block(nc, *args)
    r = run_bass_kernel_spmd(nc, [arrays], core_ids=[0])
    return r.results[0]["out"]
```
